# Optimizing a Trainium2 kernel written in Bass

```python
import numpy as np
import jax
import jax.numpy as jnp

def _softmax(x, axis=-1):
    return jax.nn.softmax(x, axis=axis)
def _gelu(x):
    return jax.nn.gelu(x, approximate=True)
def _silu(x):
    return jax.nn.silu(x)
def _sigmoid(x):
    return jax.nn.sigmoid(x)
def _layernorm(x, axis=-1, eps=1e-5):
    m = jnp.mean(x, axis=axis, keepdims=True)
    v = jnp.var(x, axis=axis, keepdims=True)
    return (x - m) / jnp.sqrt(v + eps)
def _scatter_add(tgt, idx, src, axis=0):
    return tgt.at[idx].add(src)
def _segment_sum(src, seg, n):
    return jax.ops.segment_sum(src, seg, n)

kernel_name = 'mk_adj_preln_d2_adj_512_18b143'

def setup_inputs(seed: int = 0):
    np.random.seed(seed)
    _w = jnp.asarray
    def _rec_inputs():
        import jax
        import jax.numpy as jnp
        _gk = jax.random.key(seed)
        x = -0.0005207 + 1.001 * jax.random.normal(jax.random.fold_in(_gk, 1), (4096, 512), jnp.float32)
        _a = jax.random.bernoulli(jax.random.fold_in(_gk, 2), 0.00195312, (4096, 4096))
        adj = _a.astype(jnp.int32)
        return x, adj
    x, adj = _rec_inputs()
    def _L0_gnn_setup():
        import jax, jax.numpy as jnp
        import numpy as np
        ALPHA = 0.2
        NEG_FILL = -9000000000000000.0
        key = jax.random.key(seed)
        k1, k2, k3, k4 = jax.random.split(key, 4)
        N, D, H, F = (4096, 512, 8, 64)
        h = jax.random.normal(k1, (N, D), dtype=jnp.float32)
        adj = jax.random.randint(k2, (N, N), 0, 2, dtype=jnp.int32)
        W = jax.random.normal(k3, (H, D, F), dtype=jnp.float32) * (1.0 / np.sqrt(D))
        a = jax.random.normal(k4, (H, 2 * F), dtype=jnp.float32) * 0.1
        return {'h': h, 'adj': adj, 'W': W, 'a': a}
    _L0_gnn_all = _L0_gnn_setup()
    _L0_gnn_in = {k: v for k, v in _L0_gnn_all.items() if k in ('W', 'a', )}
    del _L0_gnn_all

    def _L1_gnn_setup():
        import jax, jax.numpy as jnp
        import numpy as np
        HEAD_SIZE = 8
        QK_DIM = 512
        V_DIM = 512
        N = 4096
        ATT_DIM = QK_DIM // HEAD_SIZE
        SCALE = ATT_DIM ** (-0.5)
        NEG_FILL = jnp.float32(-9000000000000000.0)
        key = jax.random.key(seed)
        k1, k2, k3, k4 = jax.random.split(key, 4)
        x1 = jax.random.normal(k1, (N, QK_DIM), dtype=jnp.float32)
        x2 = jax.random.normal(k2, (N, QK_DIM), dtype=jnp.float32)
        v = jax.random.normal(k3, (N, V_DIM), dtype=jnp.float32)
        adj = jax.random.randint(k4, (N, N), 0, 2, dtype=jnp.int32)
        return {'x1': x1, 'x2': x2, 'v': v, 'adj': adj}
    _L1_gnn_all = _L1_gnn_setup()
    _L1_gnn_in = {k: v for k, v in _L1_gnn_all.items() if k in ('x2', 'v', )}
    del _L1_gnn_all

    return {
        "x": x,
        "adj": adj,
        "L0_gnn_W": _L0_gnn_in["W"],
        "L0_gnn_a": _L0_gnn_in["a"],
        "L1_gnn_x2": _L1_gnn_in["x2"],
        "L1_gnn_v": _L1_gnn_in["v"],
    }

def reference(x, adj, L0_gnn_W, L0_gnn_a, L1_gnn_x2, L1_gnn_v):
    import jax
    import jax.numpy as jnp
    def _L0_gnn_ref(h, adj, W, a):
        import jax, jax.numpy as jnp
        import numpy as np
        ALPHA = 0.2
        NEG_FILL = -9000000000000000.0
        H, D, F = W.shape
        N = h.shape[0]
        hp = jnp.einsum('nd,hdf->hnf', h, W)
        a_src, a_dst = (a[:, :F], a[:, F:])
        f_src = jnp.einsum('hnf,hf->hn', hp, a_src)
        f_dst = jnp.einsum('hnf,hf->hn', hp, a_dst)
        e = jax.nn.leaky_relu(f_src[:, :, None] + f_dst[:, None, :], ALPHA)
        e = jnp.where(adj[None] > 0, e, NEG_FILL)
        att = jax.nn.softmax(e, axis=-1)
        out = jnp.einsum('hij,hjf->hif', att, hp)
        out = jnp.transpose(out, (1, 0, 2)).reshape(N, H * F)
        return jax.nn.elu(out)

    def _L1_gnn_ref(x1, x2, v, adj):
        import jax, jax.numpy as jnp
        import numpy as np
        HEAD_SIZE = 8
        QK_DIM = 512
        V_DIM = 512
        N = 4096
        ATT_DIM = QK_DIM // HEAD_SIZE
        SCALE = ATT_DIM ** (-0.5)
        NEG_FILL = jnp.float32(-9000000000000000.0)
        n = x1.shape[0]
        q = x1.reshape(n, HEAD_SIZE, -1).transpose(1, 0, 2) * SCALE
        k = x2.reshape(n, HEAD_SIZE, -1).transpose(1, 0, 2)
        vv = v.reshape(n, HEAD_SIZE, -1).transpose(1, 0, 2)
        scores = jnp.einsum('hnd,hmd->hnm', q, k)
        scores = jnp.where(adj > 0, scores, NEG_FILL)
        attn = jax.nn.softmax(scores, axis=-1)
        out = jnp.einsum('hnm,hmd->hnd', attn, vv)
        return out.transpose(1, 0, 2).reshape(n, -1)

    h = jnp.maximum(_layernorm(x, axis=-1), 0.0)
    x = x + _L0_gnn_ref(h, adj, L0_gnn_W, L0_gnn_a)
    h = jnp.maximum(_layernorm(x, axis=-1), 0.0)
    x = x + _L1_gnn_ref(h, L1_gnn_x2, L1_gnn_v, adj)
    return x


_drawn_inputs = setup_inputs


def setup_inputs(seed=0):
    import zlib

    import numpy as np

    out = dict(_drawn_inputs(seed))
    spreads = {}
    factors = {}
    for name, (base, spread) in spreads.items():
        noise = np.random.default_rng([zlib.crc32(name.encode()), seed]).standard_normal(out[name].shape)
        drawn = base * np.exp(spread * noise) if base else spread * noise
        out[name] = jnp.asarray(drawn.astype(out[name].dtype))
    for name, factor in factors.items():
        out[name] = (out[name] * factor).astype(out[name].dtype)
    return out
```

```python
from contextlib import ExitStack

import concourse.bass as bass
from concourse import mybir

FP32 = mybir.dt.float32
I32 = mybir.dt.int32
ALU = mybir.AluOpType
ACT = mybir.ActivationFunctionType
AX = mybir.AxisListType

P = 128
N = 4096
D = 512
H = 8
F = D // H
T = N // P
ROW = D + H
BLK = 512
NB = N // BLK
SCALE = float(F) ** -0.5
ALPHA = 0.2
EPS = 1e-5
BIG = 3.0e38
NEG_FILL = -9.0e15


def hold(engine, tally, sem, value):
    engine.wait_ge(sem, value)
    engine.sem_inc(tally, 1)


def graph_layers(nc, x, adj, kv, w, a, eye, out):
    table = nc.dram_tensor("projected", (N, ROW), FP32).ap()
    x_t = x.rearrange("(t p) d -> p t d", p=P)
    out_t = out.rearrange("(t p) d -> p t d", p=P)
    adj_t = adj.rearrange("(t p) n -> p t n", p=P)
    table_t = table.rearrange("(t p) d -> p t d", p=P)
    kv_t = kv.rearrange("(t p) (k h f) -> p t k h f", p=P, k=2, h=H)

    ctx = ExitStack()
    with ctx:
        def sb(name, shape, dt=FP32):
            return ctx.enter_context(nc.sbuf_tensor(name, shape, dt))

        def sem(name):
            return ctx.enter_context(nc.semaphore(name))

        bank = [ctx.enter_context(nc.psum_tensor(f"bank{i}", [P, BLK], FP32)) for i in range(8)]
        ident = sb("ident", [P, P])
        eps_c = sb("eps_c", [P, 1])
        f_src = sb("f_src", [P, T, H])
        held = {e: sem(f"held_{e}") for e in ("pe", "dve")}

        with ExitStack() as own:
            def sbp(name, shape, dt=FP32):
                return own.enter_context(nc.sbuf_tensor(name, shape, dt))

            def semp(name):
                return own.enter_context(nc.semaphore(name))

            NC_ = D // P
            wa = sbp("wa", [P, NC_, D + 2 * H])
            a_bc = sbp("a_bc", [P, H, 2, F])
            wprod = sbp("wprod", [P, D])
            xb = sbp("xb", [P, 2, D])
            hb = sbp("hb", [P, 2, D])
            hT = sbp("hT", [P, 2, D])
            rowb = sbp("rowb", [P, 2, ROW])
            st = sbp("st", [P, 2, 6])
            mv = sbp("mv", [P, 2, 2])
            lnv = sbp("lnv", [P, 2, 1])
            rstd = sbp("rstd", [P, 2, 1])
            nbias = sbp("nbias", [P, 2, 1])
            ps_t, ps_h, ps_f = bank[0:2], bank[2:4], bank[4:6]

            consts_in = semp("consts_in")
            x_in = [semp(f"x_in{p}") for p in range(2)]
            wprod_done = semp("wprod_done")
            wa_done = semp("wa_done")
            wa_read = semp("wa_read")
            stats = semp("stats")
            stats_chain = semp("stats_chain")
            ln_done = semp("ln_done")
            rstd_done = semp("rstd_done")
            nbias_done = semp("nbias_done")
            h_done = semp("h_done")
            tr_done = semp("tr_done")
            hT_done = semp("hT_done")
            proj_done = semp("proj_done")
            hp_copied = semp("hp_copied")
            fd_copied = semp("fd_copied")
            fs_done = semp("fs_done")
            stored = [semp(f"stored{p}") for p in range(2)]

            with nc.Block() as block:
                @block.sync
                def _(sp):
                    sp.dma_start(ident[:], eye).then_inc(consts_in, 16)
                    sp.dma_start(wa[:, :, 0:D], w.rearrange("(c p) n -> p c n", p=P)).then_inc(consts_in, 16)
                    sp.dma_start(a_bc[:].rearrange("p h s f -> p (h s f)"),
                                 a.rearrange("(o h) f -> o (h f)", o=1).to_broadcast((P, 2 * D))
                                 ).then_inc(consts_in, 16)
                    for p in range(2):
                        sp.sem_inc(stored[p], 1)
                        sp.dma_start(xb[:, p, :], x_t[:, p, :]).then_inc(x_in[p], 16)

                    def store(k, p):
                        sp.wait_ge(hp_copied, k + 3)
                        sp.wait_ge(fd_copied, k + 3)
                        sp.dma_start(table_t[:, k, :], rowb[:, p, :]).then_inc(stored[p], 16)

                    with sp.Fori(1, T // 2) as i:
                        t = i * 2
                        for p in range(2):
                            sp.wait_ge(h_done, t + p - 1)
                            sp.dma_start(xb[:, p, :], x_t[:, t + p, :]).then_inc(x_in[p], 16)
                            store(t + p - 2, p)
                    for p in range(2):
                        store(T - 2 + p, p)
                        sp.wait_ge(stored[p], 16 * T // 2 + 1)

                @block.vector
                def _(dve):
                    dve.sem_inc(fd_copied, 2)
                    dve.memset(eps_c[:], EPS).then_inc(stats_chain, 1)
                    dve.wait_ge(consts_in, 48)
                    for c in range(NC_):
                        for s in range(2):
                            n = 2 * c + s
                            if n:
                                dve.wait_ge(wa_done, n)
                            dve.tensor_tensor(wprod[:].rearrange("p (h f) -> p h f", h=H),
                                              wa[:, c, 0:D].rearrange("p (h f) -> p h f", h=H),
                                              a_bc[:, :, s, :], ALU.mult).then_inc(wprod_done, 1)
                            dve.wait_ge(wprod_done, n + 1)
                            dve.tensor_reduce(wa[:, c, D + s * H:D + (s + 1) * H],
                                              wprod[:].rearrange("p (h f) -> p h f", h=H),
                                              AX.X, ALU.add).then_inc(wa_done, 1)
                    with dve.Fori(0, T // 2) as i:
                        t = i * 2
                        for p in range(2):
                            k = t + p
                            dve.wait_ge(x_in[p], 8 * t + 16)
                            dve.bn_stats(st[:, p, :], xb[:, p, :]).then_inc(stats, 1)
                            hold(dve, held["dve"], stats, 2 * k + 1)
                            dve.bn_aggr(mv[:, p, :], st[:, p, :]).then_inc(stats, 1)
                            dve.wait_ge(rstd_done, k + 1)
                            dve.wait_ge(stats, 2 * k + 2)
                            dve.tensor_scalar(nbias[:, p, :], mv[:, p, 0:1], rstd[:, p, :], -1.0,
                                              ALU.mult, ALU.mult).then_inc(nbias_done, 1)
                            dve.wait_ge(proj_done, k + 1)
                            dve.tensor_copy(f_src[:, k, :], ps_f[p][:, 0:H]).then_inc(fs_done, 1)
                            dve.wait_ge(stored[p], 8 * t + 1)
                            dve.tensor_copy(rowb[:, p, D:ROW], ps_f[p][:, H:2 * H]).then_inc(fd_copied, 1)

                @block.scalar
                def _(act):
                    act.sem_inc(hp_copied, 2)
                    act.wait_ge(stats_chain, 1)
                    with act.Fori(0, T // 2) as i:
                        t = i * 2
                        for p in range(2):
                            k = t + p
                            act.wait_ge(stats, 2 * k + 2)
                            act.activation(lnv[:, p, :], mv[:, p, 1:2], ACT.Ln, bias=eps_c[:]).then_inc(ln_done, 1)
                            act.wait_ge(ln_done, k + 1)
                            act.activation(rstd[:, p, :], lnv[:, p, :], ACT.Exp, scale=-0.5).then_inc(rstd_done, 1)
                            act.wait_ge(nbias_done, k + 1)
                            act.activation(hb[:, p, :], xb[:, p, :], ACT.Relu, bias=nbias[:, p, :],
                                           scale=rstd[:, p, :]).then_inc(h_done, 1)
                            act.wait_ge(tr_done, k + 1)
                            act.activation(hT[:, p, :], ps_t[p][:], ACT.Copy).then_inc(hT_done, 1)
                            act.wait_ge(proj_done, k + 1)
                            act.wait_ge(stored[p], 8 * t + 1)
                            act.activation(rowb[:, p, 0:D], ps_h[p][:], ACT.Copy).then_inc(hp_copied, 1)

                @block.tensor
                def _(pe):
                    pe.wait_ge(consts_in, 48)
                    pe.wait_ge(wa_done, 2 * NC_)
                    with pe.Fori(0, T // 2) as i:
                        t = i * 2
                        for p in range(2):
                            k = t + p
                            pe.wait_ge(h_done, k + 1)
                            for c in range(NC_):
                                last = pe.transpose(ps_t[p][:, c * P:(c + 1) * P], hb[:, p, c * P:(c + 1) * P],
                                                    ident[:])
                            last.then_inc(tr_done, 1)
                            pe.wait_ge(hT_done, k + 1)
                            pe.wait_ge(hp_copied, k + 1)
                            pe.wait_ge(fd_copied, k + 1)
                            for c in range(NC_):
                                pe.matmul(ps_h[p][:], hT[:, p, c * P:(c + 1) * P], wa[:, c, 0:D],
                                          start=c == 0, stop=c == NC_ - 1)
                            for c in range(NC_):
                                last = pe.matmul(ps_f[p][:, 0:2 * H], hT[:, p, c * P:(c + 1) * P],
                                                 wa[:, c, D:D + 2 * H], start=c == 0, stop=c == NC_ - 1)
                            last.then_inc(proj_done, 1)

        dense_layers(nc, x_t, adj_t, table_t, kv_t, out_t, bank, ident, eps_c, f_src, held)


def dense_layers(nc, x_t, adj_t, table_t, kv_t, out_t, bank, ident, eps_c, f_src, held):
    ctx = ExitStack()
    with ctx:
        def sb(name, shape, dt=FP32):
            return ctx.enter_context(nc.sbuf_tensor(name, shape, dt))

        def sem(name):
            return ctx.enter_context(nc.semaphore(name))

        hp = sb("g_hp", [P, T, ROW])
        kvh = sb("g_kvh", [P, T, 2, F])
        val = sb("g_val", [P, T, F])
        fdc = sb("g_fdc", [P, T])
        fill = sb("g_fill", [P, N])
        adj_b = fill[:].bitcast(I32)
        e = sb("g_e", [P, N])
        pT = sb("g_pT", [P, N])
        kT = pT
        x0 = sb("g_x0", [P, D])
        o = sb("g_o", [P, D])
        t0 = sb("g_t0", [P, D])
        t0n = sb("g_t0n", [P, D])
        t0e = sb("g_t0e", [P, D])
        h1 = sb("g_h1", [P, D])
        q = sb("g_q", [P, F])
        qT = sb("g_qT", [F, P])
        st = sb("g_st", [P, 6])
        mv = sb("g_mv", [P, 2])
        lnv = sb("g_lnv", [P, 1])
        rstd = sb("g_rstd", [P, 1])
        nb = sb("g_nb", [P, 1])
        nm = sb("g_nm", [P, 1])
        den = sb("g_den", [P, 1])
        rden = sb("g_rden", [P, 1])
        ps_e, ps_t, ps_o = bank[0:2], bank[2:4], bank[4]
        ps_q = bank[5]

        table_in = sem("g_table_in")
        xa_in = sem("g_xa_in")
        fill_done = sem("g_fill_done")
        row = sem("g_row")
        tile_done = sem("g_tile_done")
        out_stored = sem("g_out_stored")
        elu_neg = sem("g_elu_neg")
        elu_exp = sem("g_elu_exp")
        acc0 = sem("g_acc0")
        x1_done = sem("g_x1_done")
        stats = sem("g_stats")
        lnd = sem("g_lnd")
        rstd_done = sem("g_rstd_done")
        nb_done = sem("g_nb_done")
        h1_done = sem("g_h1_done")

        names = ("head", "kv_in", "kT_ps", "kT", "qT_ps", "qT", "block", "read", "leaky", "masked",
                 "top", "shift", "exp", "pT_ps", "pT", "weighted", "rden", "out")
        s0, s1 = [{n: sem(f"g{layer}_{n}") for n in names} for layer in range(2)]

        with nc.Block() as block:
            @block.sync
            def _(sp):
                sp.dma_start(hp[:], table_t).then_inc(table_in, 16)
                sp.sem_inc(out_stored, 1)
                with sp.Fori(0, T) as g:
                    sp.wait_ge(tile_done, g + 1)
                    sp.dma_start(x0[:], x_t[:, g, :]).then_inc(xa_in, 16)
                    sp.dma_start(adj_b, adj_t[:, g, :]).then_inc(xa_in, 16)
                    with sp.Fori(0, H) as h:
                        sp.wait_ge(s1["weighted"], g * H + h + 1)
                        for k in range(2):
                            sp.dma_start(kvh[:, :, k, :], kv_t[:, :, k, h, :]).then_inc(s1["kv_in"], 16)
                    sp.wait_ge(tile_done, g + 2)
                    sp.dma_start(out_t[:, g, :], t0[:]).then_inc(out_stored, 16)
                sp.wait_ge(out_stored, 16 * T + 1)

            @block.vector
            def _(dve):
                dve.sem_inc(tile_done, 1)
                dve.sem_inc(s0["out"], 1)
                dve.sem_inc(s1["out"], 1)
                dve.wait_ge(table_in, 16)

                def attend(s, u, h):
                    dve.scalar_tensor_tensor(e[:], fill[:], NEG_FILL, e[:], ALU.add, ALU.min
                                             ).then_inc(s["masked"], 1)
                    dve.wait_ge(s["masked"], u + 1)
                    dve.reduce_max(nm[:], e[:], AX.X).then_inc(s["top"], 1)
                    dve.wait_ge(s["top"], u + 1)
                    dve.tensor_scalar(nm[:], nm[:], -1.0 if s is s0 else -SCALE, None, ALU.mult
                                      ).then_inc(s["shift"], 1)
                    dve.wait_ge(s["exp"], u + 1)
                    dve.reciprocal(rden[:], den[:]).then_inc(s["rden"], 1)
                    dve.wait_ge(s["rden"], u + 1)
                    dve.wait_ge(s["weighted"], u + 2)
                    dve.tensor_scalar(o[:, bass.ds(h * F, F)], ps_o[:, 0:F], rden[:], None, ALU.mult
                                      ).then_inc(s["out"], 1)

                with dve.Fori(0, T) as g:
                    dve.wait_ge(xa_in, 32 * g + 32)
                    dve.tensor_scalar(fill[:], adj_b, 0.0, BIG, ALU.is_gt, ALU.mult).then_inc(fill_done, 1)
                    with dve.Fori(0, H) as h:
                        u = g * H + h
                        dve.wait_ge(s0["weighted"], u + 1)
                        dve.tensor_copy(val[:], hp[:, :, bass.ds(h * F, F)]).then_inc(s0["head"], 1)
                        dve.tensor_copy(fdc[:], hp[:, :, bass.ds(h + D, 1)].rearrange("p t o -> p (t o)")
                                        ).then_inc(s0["head"], 1)
                        for b in range(NB):
                            dve.wait_ge(s0["block"], u * NB + b + 1)
                            dve.tensor_scalar(e[:, b * BLK:(b + 1) * BLK], ps_e[b % 2][:],
                                              f_src[:, g, bass.ds(h, 1)], None, ALU.add
                                              ).then_inc(s0["read"], 1)
                        dve.wait_ge(s0["read"], u * NB + NB + 2)
                        dve.scalar_tensor_tensor(e[:], e[:], ALPHA, e[:], ALU.mult, ALU.max
                                                 ).then_inc(s0["leaky"], 1)
                        dve.wait_ge(s0["leaky"], u + 1)
                        dve.wait_ge(fill_done, g + 1)
                        attend(s0, u, h)
                    dve.wait_ge(elu_exp, g + 1)
                    dve.wait_ge(out_stored, 16 * g + 1)
                    dve.scalar_tensor_tensor(t0[:], o[:], 0.0, t0e[:], ALU.max, ALU.add).then_inc(acc0, 1)
                    dve.wait_ge(acc0, g + 1)
                    dve.scalar_tensor_tensor(x0[:], t0[:], -1.0, x0[:], ALU.add, ALU.add).then_inc(x1_done, 1)
                    dve.wait_ge(x1_done, g + 1)
                    dve.bn_stats(st[:], x0[:]).then_inc(stats, 1)
                    hold(dve, held["dve"], stats, 2 * g + 1)
                    dve.bn_aggr(mv[:], st[:]).then_inc(stats, 1)
                    dve.wait_ge(stats, 2 * g + 2)
                    dve.wait_ge(rstd_done, g + 1)
                    dve.tensor_scalar(nb[:], mv[:, 0:1], rstd[:], -1.0, ALU.mult, ALU.mult).then_inc(nb_done, 1)
                    hold(dve, held["dve"], h1_done, g + 1)
                    with dve.Fori(0, H) as h:
                        u = g * H + h
                        dve.wait_ge(s1["weighted"], u + 1)
                        dve.tensor_copy(q[:], h1[:, bass.ds(h * F, F)]).then_inc(s1["head"], 1)
                        for b in range(NB):
                            dve.wait_ge(s1["block"], u * NB + b + 1)
                            dve.tensor_copy(e[:, b * BLK:(b + 1) * BLK], ps_e[b % 2][:]).then_inc(s1["read"], 1)
                        dve.wait_ge(s1["read"], u * NB + NB + 2)
                        attend(s1, u, h)
                    dve.wait_ge(s1["out"], (g + 1) * H + 1)
                    dve.tensor_tensor(t0[:], o[:], x0[:], ALU.add).then_inc(tile_done, 1)

            @block.scalar
            def _(act):
                def attend(s, u):
                    act.wait_ge(s["shift"], u + 1)
                    act.activation(e[:], e[:], ACT.Exp, bias=nm[:], scale=1.0 if s is s0 else SCALE,
                                   accum_out=den[:]).then_inc(s["exp"], 1)
                    for b in range(NB):
                        act.wait_ge(s["pT_ps"], u * NB + b + 1)
                        act.activation(pT[:, b * BLK:(b + 1) * BLK], ps_t[b % 2][:], ACT.Copy
                                       ).then_inc(s["pT"], 1)

                for s in (s0, s1):
                    act.sem_inc(s["pT"], 2)
                act.sem_inc(s1["kT"], 2)
                with act.Fori(0, T) as g:
                    with act.Fori(0, H) as h:
                        attend(s0, g * H + h)
                    act.wait_ge(s0["out"], (g + 1) * H + 1)
                    act.activation(t0n[:], o[:], ACT.Relu, scale=-1.0).then_inc(elu_neg, 1)
                    act.wait_ge(elu_neg, g + 1)
                    act.activation(t0e[:], t0n[:], ACT.Exp, scale=-1.0).then_inc(elu_exp, 1)
                    act.wait_ge(stats, 2 * g + 2)
                    act.activation(lnv[:], mv[:, 1:2], ACT.Ln, bias=eps_c[:]).then_inc(lnd, 1)
                    act.wait_ge(lnd, g + 1)
                    act.activation(rstd[:], lnv[:], ACT.Exp, scale=-0.5).then_inc(rstd_done, 1)
                    act.wait_ge(nb_done, g + 1)
                    act.activation(h1[:], x0[:], ACT.Relu, bias=nb[:], scale=rstd[:]).then_inc(h1_done, 1)
                    with act.Fori(0, H) as h:
                        u = g * H + h
                        act.wait_ge(s1["qT_ps"], u + 1)
                        act.activation(qT[:], ps_q[0:F, 0:P], ACT.Copy).then_inc(s1["qT"], 1)
                        for b in range(NB):
                            act.wait_ge(s1["kT_ps"], u * NB + b + 1)
                            act.activation(kT[0:F, b * BLK:(b + 1) * BLK], ps_t[b % 2][0:F, :], ACT.Copy
                                           ).then_inc(s1["kT"], 1)
                        attend(s1, u)

            @block.tensor
            def _(pe):
                PB = BLK // P
                for s in (s0, s1):
                    pe.sem_inc(s["weighted"], 1)
                pe.wait_ge(table_in, 16)

                def attend(s, u, values):
                    pe.wait_ge(s["exp"], u + 1)
                    for b in range(NB):
                        pe.wait_ge(s["pT"], u * NB + b + 1)
                        for c in range(PB):
                            j = b * PB + c
                            last = pe.transpose(ps_t[b % 2][:, c * P:(c + 1) * P], e[:, j * P:(j + 1) * P], ident[:])
                        last.then_inc(s["pT_ps"], 1)
                    pe.wait_ge(s["pT"], u * NB + NB + 2)
                    pe.wait_ge(s["out"], u + 1)
                    for j in range(T):
                        last = pe.matmul(ps_o[:, 0:F], pT[:, j * P:(j + 1) * P], values(j),
                                         start=j == 0, stop=j == T - 1)
                    last.then_inc(s["weighted"], 1)

                with pe.Fori(0, T) as g:
                    with pe.Fori(0, H) as h:
                        u = g * H + h
                        pe.wait_ge(s0["head"], 2 * u + 2)
                        for b in range(NB):
                            pe.wait_ge(s0["read"], u * NB + b + 1)
                            for c in range(PB):
                                j = b * PB + c
                                last = pe.matmul(ps_e[b % 2][:, c * P:(c + 1) * P],
                                                 fdc[:, j:j + 1].to_broadcast((P, P)), ident[:],
                                                 start=True, stop=True)
                            last.then_inc(s0["block"], 1)
                        attend(s0, u, lambda j: val[:, j, :])
                    with pe.Fori(0, H) as h:
                        u = g * H + h
                        hold(pe, held["pe"], s1["head"], u + 1)
                        pe.transpose(ps_q[0:F, 0:P], q[:], ident[:]).then_inc(s1["qT_ps"], 1)
                        pe.wait_ge(s1["kv_in"], 32 * u + 32)
                        for b in range(NB):
                            hold(pe, held["pe"], s1["kT"], u * NB + b + 1)
                            for c in range(PB):
                                j = b * PB + c
                                last = pe.transpose(ps_t[b % 2][0:F, c * P:(c + 1) * P], kvh[:, j, 0, :], ident[:])
                            last.then_inc(s1["kT_ps"], 1)
                        pe.wait_ge(s1["qT"], u + 1)
                        for b in range(NB):
                            pe.wait_ge(s1["kT"], u * NB + b + 3)
                            pe.wait_ge(s1["read"], u * NB + b + 1)
                            pe.matmul(ps_e[b % 2][:], qT[:], kT[0:F, b * BLK:(b + 1) * BLK],
                                      start=True, stop=True).then_inc(s1["block"], 1)
                        attend(s1, u, lambda j: kvh[:, j, 1, :])

            @block.gpsimd
            def _(pool):
                pool.sem_inc(s0["read"], 2)
                pool.sem_inc(s1["read"], 2)


def kernel(x, adj, L0_gnn_W, L0_gnn_a, L1_gnn_x2, L1_gnn_v):
    import numpy as np
    import concourse.bacc as bacc
    from concourse.bass_utils import run_bass_kernel_spmd

    arrays = {
        "x": np.ascontiguousarray(x),
        "adj": np.ascontiguousarray(adj),
        "kv": np.concatenate([L1_gnn_x2, L1_gnn_v], axis=1),
        "w": np.ascontiguousarray(np.transpose(L0_gnn_W, (1, 0, 2)).reshape(D, D)),
        "a": np.ascontiguousarray(L0_gnn_a),
        "eye": np.eye(P, dtype=np.float32),
    }
    nc = bacc.Bacc("TRN2", target_bir_lowering=False, num_devices=1)
    args = {n: nc.dram_tensor(n, v.shape, mybir.dt.from_np(v.dtype), kind="ExternalInput").ap()
            for n, v in arrays.items()}
    out = nc.dram_tensor("out", (N, D), FP32, kind="ExternalOutput").ap()
    graph_layers(nc, **args, out=out)
    r = run_bass_kernel_spmd(nc, [arrays], core_ids=[0])
    return r.results[0]["out"]
```

```python
from contextlib import ExitStack

import concourse.bass as bass
from concourse import mybir

FP32 = mybir.dt.float32
BF16 = mybir.dt.bfloat16
I32 = mybir.dt.int32
U32 = mybir.dt.uint32
ALU = mybir.AluOpType
ACT = mybir.ActivationFunctionType
AX = mybir.AxisListType

P = 128
N = 4096
D = 512
H = 8
F = D // H
T = N // P
ROW = D + H
BLK = 512
NB = N // BLK
SCALE = float(F) ** -0.5
ALPHA = 0.2
EPS = 1e-5
BIG = 3.0e38
SEG = 512
NS = N // SEG
TOP = 8
S = 24
SLOT_COUNTS = (4, 2, 2, 2, 2, 4, 4, 4)
CHUNKS = [(sum(SLOT_COUNTS[:c]), m) for c, m in enumerate(SLOT_COUNTS)]
TWIN = 4
LN_EXP_SET = 6
NO_NODE = 2 * N
REC = 36
R_COUNT, R_ROW, R_FSRC = S, S + 1, S + 4
NDEG = S + 1
NEG_FILL = -9.0e15


def hold(engine, tally, sem, value):
    engine.wait_ge(sem, value)
    engine.sem_inc(tally, 1)


def load_exp_and_ln(nc, act):
    act.add_instruction(mybir.InstLoadActFuncSet(act_func_set_id=LN_EXP_SET, name=nc.get_next_instruction_name(),
                                                 engine=act.engine))


def when(engine, sem, value):
    if not isinstance(value, int) or value > 0:
        engine.wait_ge(sem, value)


def hold_when(engine, tally, sem, value):
    if not isinstance(value, int) or value > 0:
        hold(engine, tally, sem, value)


def graph_layers(nc, x, adj, kv, w, a, eye, before, seg_base, degrees, row_index, tile_key, out):
    table = nc.dram_tensor("projected", (N, ROW), FP32).ap()
    records = nc.dram_tensor("records", (N, REC), I32).ap()
    x_t = x.rearrange("(t p) d -> p t d", p=P)
    out_t = out.rearrange("(t p) d -> p t d", p=P)
    adj_t = adj.rearrange("(t p) n -> p t n", p=P)
    table_t = table.rearrange("(t p) d -> p t d", p=P)
    kv_t = kv.rearrange("(t p) (k h f) -> p t k h f", p=P, k=2, h=H)
    v_t = kv.rearrange("(t p) (k d) -> p t k d", p=P, k=2)

    ctx = ExitStack()
    with ctx:
        def sb(name, shape, dt=FP32):
            return ctx.enter_context(nc.sbuf_tensor(name, shape, dt))

        def sem(name):
            return ctx.enter_context(nc.semaphore(name))

        psum = ctx.enter_context(nc.psum_tensor("psum", [P, 8, BLK], FP32))
        bank = [psum[:, i, :] for i in range(8)]
        ident = sb("ident", [P, P])
        eps_c = sb("eps_c", [P, 1])
        f_src = sb("f_src", [P, T, H])
        found = sb("found", [P, T, S + 1])
        mean_hp = sb("mean_hp", [P, D])
        mean_v = sb("mean_v", [P, D])
        flagged = sb("flagged", [1, T], I32)
        n_flagged = sb("n_flagged", [1, 1], I32)
        held = {e: sem(f"held_{e}") for e in ("pe", "dve", "pool", "sp")}

        project_and_scan(nc, x_t, adj_t, v_t, table_t, w, a, eye, seg_base, bank, ident, eps_c, f_src,
                         found, mean_hp, mean_v, held)
        with ExitStack() as slots:
            g0 = slots.enter_context(nc.sbuf_tensor("g0", [P, S + TWIN, ROW], FP32))
            gkv = slots.enter_context(nc.sbuf_tensor("gkv", [P, S + TWIN, 2, D], FP32))
            sort_rows(nc, records, before, degrees, row_index, tile_key, bank, f_src, found, flagged,
                      n_flagged, g0, gkv)
            sparse_layers(nc, x, kv, table, records, out, psum, ident, eps_c, found, mean_hp, mean_v, held,
                          g0, gkv)
        dense_layers(nc, x_t, adj_t, table_t, kv_t, out_t, bank, ident, eps_c, f_src, held, flagged, n_flagged)


def project_and_scan(nc, x_t, adj_t, v_t, table_t, w, a, eye, seg_base_in, bank, ident, eps_c, f_src,
                     found, mean_hp, mean_v, held):
    with ExitStack() as own:
        def sb(name, shape, dt=FP32):
            return own.enter_context(nc.sbuf_tensor(name, shape, dt))

        mine = []

        def sem(name):
            mine.append(nc.alloc_semaphore(name))
            return mine[-1]

        ND = D // P
        wa = sb("wa", [P, ND, D + 2 * H])
        a_bc = sb("a_bc", [P, H, 2, F])
        wprod = sb("wprod", [P, D])
        xb = sb("xb", [P, 2, D])
        vb = sb("vb", [P, 2, D])
        hb = sb("hb", [P, 2, D])
        hT = sb("hT", [P, 2, D])
        rowb = sb("rowb", [P, 2, ROW])
        st = sb("st", [P, 2, 6])
        mv = sb("mv", [P, 2, 2])
        negm = sb("negm", [P, 2, 1])
        lnv = sb("lnv", [P, 2, 1])
        rstd = sb("rstd", [P, 2, 1])
        nbias = sb("nbias", [P, 2, 1])
        adjb = sb("adjb", [P, 2, N], I32)
        mask = sb("mask", [P, 2, NS, SEG + TOP], BF16)
        ones8 = sb("ones8", [P, TOP], BF16)
        nth = sb("nth", [P, 2, NS * TOP], U32)
        base = sb("base", [P, NS * TOP])
        key = sb("key", [P, 2, NS * TOP])
        rest = sb("rest", [P, 2, NS * TOP])
        first = sb("first", [P, 2, S])
        share = sb("share", [P, 1])
        zero = sb("zero", [P, P])
        meanT = sb("meanT", [P, 2 * ND])
        ps_t, ps_h, ps_f = bank[0:2], bank[2:4], bank[4:6]
        ps_m, ps_b = bank[6], bank[7]

        consts_in = sem("consts_in")
        x_in = [sem(f"x_in{p}") for p in range(2)]
        v_in = [sem(f"v_in{p}") for p in range(2)]
        adj_in = [sem(f"adj_in{p}") for p in range(2)]
        sets = sem("sets")
        wprod_done = sem("wprod_done")
        wa_done = sem("wa_done")
        stats = sem("stats")
        ln_chain = sem("ln_chain")
        h_done = sem("h_done")
        tr_done = sem("tr_done")
        hT_done = sem("hT_done")
        proj_done = sem("proj_done")
        hp_copied = sem("hp_copied")
        v_summed = sem("v_summed")
        mask_done = sem("mask_done")
        scanned = sem("scanned")
        compact = sem("compact")
        first_kept = sem("first_kept")
        meanT_ps = sem("meanT_ps")
        meanT_done = sem("meanT_done")
        means_ps = sem("means_ps")
        stored = [sem(f"stored{p}") for p in range(2)]
        NCONST = 4
        LINKS = 2 + 2 * S // TOP - 1

        with nc.Block() as block:
            @block.sync
            def _(sp):
                sp.dma_start(ident[:], eye).then_inc(consts_in, 16)
                sp.dma_start(base[:], seg_base_in).then_inc(consts_in, 16)
                sp.dma_start(wa[:, :, 0:D], w.rearrange("(c p) n -> p c n", p=P)).then_inc(consts_in, 16)
                sp.dma_start(a_bc[:].rearrange("p h s f -> p (h s f)"),
                             a.rearrange("(o h) f -> o (h f)", o=1).to_broadcast((P, 2 * D))
                             ).then_inc(consts_in, 16)

                def load(k, p):
                    when(sp, mask_done, k - 1)
                    sp.dma_start(adjb[:, p, :], adj_t[:, k, :]).then_inc(adj_in[p], 16)

                for p in range(2):
                    sp.dma_start(xb[:, p, :], x_t[:, p, :]).then_inc(x_in[p], 16)
                    load(p, p)
                with sp.Fori(1, T // 2) as i:
                    for p in range(2):
                        load(i * 2 + p, p)

            @block.gpsimd
            def _(pool):
                def load_values(k, p):
                    hold_when(pool, held["pool"], v_summed, k - 1)
                    pool.dma_start(vb[:, p, :], v_t[:, k, 1, :]).then_inc(v_in[p], 16)

                def keep(k, p):
                    pool.wait_ge(compact, LINKS * (k + 1))
                    pool.tensor_copy(found[:, k, 0:S], first[:, p, :]).then_inc(first_kept, 1)
                    hold(pool, held["pool"], hp_copied, k + 1)
                    pool.dma_start(table_t[:, k, :], rowb[:, p, :]).then_inc(stored[p], 16)

                for p in range(2):
                    load_values(p, p)
                with pool.Fori(1, T // 2) as i:
                    for p in range(2):
                        load_values(i * 2 + p, p)
                        keep(i * 2 + p - 2, p)
                for p in range(2):
                    keep(T - 2 + p, p)
                    pool.wait_ge(stored[p], 16 * T // 2)

            @block.vector
            def _(dve):
                dve.memset(eps_c[:], EPS).then_inc(sets, 1)
                dve.memset(ones8[:], 1.0).then_inc(sets, 1)
                for p in range(2):
                    dve.memset(mask[:, p, :, SEG:SEG + TOP], 1.0).then_inc(sets, 1)
                dve.memset(share[:], 1.0 / N).then_inc(sets, 1)
                dve.memset(zero[:], 0.0).then_inc(sets, 1)
                dve.wait_ge(consts_in, 16 * NCONST)
                for c in range(ND):
                    for s in range(2):
                        n = 2 * c + s
                        if n:
                            dve.wait_ge(wa_done, n)
                        dve.tensor_tensor(wprod[:].rearrange("p (h f) -> p h f", h=H),
                                          wa[:, c, 0:D].rearrange("p (h f) -> p h f", h=H),
                                          a_bc[:, :, s, :], ALU.mult).then_inc(wprod_done, 1)
                        dve.wait_ge(wprod_done, n + 1)
                        dve.tensor_reduce(wa[:, c, D + s * H:D + (s + 1) * H],
                                          wprod[:].rearrange("p (h f) -> p h f", h=H),
                                          AX.X, ALU.add).then_inc(wa_done, 1)

                def statistics(k, p, half):
                    dve.wait_ge(x_in[p], 16 * half + 16)
                    dve.bn_stats(st[:, p, :], xb[:, p, :]).then_inc(stats, 1)
                    yield
                    hold(dve, held["dve"], stats, 3 * k + 1)
                    dve.bn_aggr(mv[:, p, :], st[:, p, :]).then_inc(stats, 1)
                    yield
                    dve.wait_ge(stats, 3 * k + 2)
                    dve.tensor_scalar(negm[:, p, :], mv[:, p, 0:1], -1.0, None, ALU.mult).then_inc(stats, 1)

                def shortlist(k, p):
                    dve.wait_ge(scanned, k + 1)
                    dve.tensor_tensor(rest[:, p, :], nth[:, p, :], base[:], ALU.add).then_inc(compact, 1)
                    yield
                    dve.wait_ge(compact, LINKS * k + 1)
                    dve.scalar_tensor_tensor(key[:, p, :], nth[:, p, :], float(SEG), rest[:, p, :],
                                             ALU.is_lt, ALU.mult).then_inc(compact, 1)
                    yield
                    hold_when(dve, held["dve"], first_kept, k - 1)
                    for r in range(S // TOP):
                        got = first[:, p, r * TOP:(r + 1) * TOP]
                        src, dst = (key, rest) if r % 2 == 0 else (rest, key)
                        hold(dve, held["dve"], compact, LINKS * k + 2 + 2 * r)
                        dve.max(got, src[:, p, :]).then_inc(compact, 1)
                        yield
                        if r + 1 < S // TOP:
                            hold(dve, held["dve"], compact, LINKS * k + 3 + 2 * r)
                            dve.match_replace(dst[:, p, :], got, src[:, p, :], 0.0).then_inc(compact, 1)
                            yield

                def scan(k, p, half, beside):
                    hold(dve, held["dve"], mask_done, k + 1)
                    for s in range(NS):
                        last = dve.max_index(nth[:, p, s * TOP:(s + 1) * TOP], ones8[:], mask[:, p, s, :])
                        if s == NS - 1:
                            last.then_inc(scanned, 1)
                        for steps in beside:
                            next(steps, None)
                    for steps in beside:
                        for _ in steps:
                            pass

                def tile(k, p, half):
                    beside = [statistics(k, p, half)]
                    if not isinstance(k, int) or k:
                        beside.append(shortlist(k - 1, 1 - p))
                    scan(k, p, half, beside)

                for p in range(2):
                    tile(p, p, 0)
                with dve.Fori(1, T // 2) as i:
                    for p in range(2):
                        tile(i * 2 + p, p, i)
                for _ in shortlist(T - 1, 1):
                    pass
                dve.wait_ge(meanT_ps, 1)
                dve.tensor_copy(meanT[:], ps_m[:, 0:2 * ND]).then_inc(meanT_done, 1)
                dve.wait_ge(means_ps, 1)
                dve.tensor_copy(mean_v[:], ps_b[:])

            @block.scalar
            def _(act):
                load_exp_and_ln(nc, act)
                act.wait_ge(sets, 6)

                def masks(k, p, half):
                    act.wait_ge(adj_in[p], 16 * half + 16)
                    when(act, scanned, k - 1)
                    act.activation(mask[:, p, :, 0:SEG], adjb[:, p, :].rearrange("p (s n) -> p s n", s=NS),
                                   ACT.Relu, accum_out=found[:, k, S:S + 1]).then_inc(mask_done, 1)

                def normalise(k, p):
                    act.wait_ge(stats, 3 * k + 3)
                    act.activation(lnv[:, p, :], mv[:, p, 1:2], ACT.Ln, bias=eps_c[:]).then_inc(ln_chain, 1)
                    act.wait_ge(ln_chain, 3 * k + 1)
                    act.activation(rstd[:, p, :], lnv[:, p, :], ACT.Exp, scale=-0.5).then_inc(ln_chain, 1)
                    act.wait_ge(ln_chain, 3 * k + 2)
                    act.activation(nbias[:, p, :], negm[:, p, :], ACT.Copy, scale=rstd[:, p, :]
                                   ).then_inc(ln_chain, 1)
                    act.wait_ge(ln_chain, 3 * k + 3)
                    act.activation(hb[:, p, :], xb[:, p, :], ACT.Relu, bias=nbias[:, p, :],
                                   scale=rstd[:, p, :]).then_inc(h_done, 1)

                def load_x(k, p):
                    when(act, h_done, k - 1)
                    act.dma_start(xb[:, p, :], x_t[:, k, :]).then_inc(x_in[p], 16)

                def keep_hp(k, p):
                    act.wait_ge(proj_done, k + 1)
                    when(act, stored[p], (k - p) * 8)
                    act.activation(f_src[:, k, :], ps_f[p][:, 0:H], ACT.Copy)
                    act.activation(rowb[:, p, D:ROW], ps_f[p][:, H:2 * H], ACT.Copy)
                    act.activation(rowb[:, p, 0:D], ps_h[p][:], ACT.Copy).then_inc(hp_copied, 1)

                def keep_hT(k, p):
                    act.wait_ge(tr_done, k + 1)
                    act.activation(hT[:, p, :], ps_t[p][:], ACT.Copy).then_inc(hT_done, 1)

                def tile(k, p, more=True):
                    normalise(k, p)
                    if more:
                        load_x(k + 2, p)
                    if not isinstance(k, int) or k:
                        keep_hp(k - 1, 1 - p)
                    keep_hT(k, p)

                masks(0, 0, 0)
                masks(1, 1, 0)
                tile(0, 0)

                def pair(i):
                    masks(i * 2, 0, i)
                    tile(i * 2 - 1, 1)
                    masks(i * 2 + 1, 1, i)
                    tile(i * 2, 0)

                pair(1)
                with act.Fori(2, T // 2 - 1) as i:
                    pair(i)
                masks(T - 2, 0, T // 2 - 1)
                tile(T - 3, 1)
                masks(T - 1, 1, T // 2 - 1)
                tile(T - 2, 0, more=False)
                tile(T - 1, 1, more=False)
                keep_hp(T - 1, 1)
                act.wait_ge(means_ps, 1)
                act.activation(mean_hp[:], ps_h[0][:], ACT.Copy)

            @block.tensor
            def _(pe):
                pe.wait_ge(consts_in, 16 * NCONST)
                pe.wait_ge(wa_done, 2 * ND)
                pe.wait_ge(sets, 6)
                pe.matmul(ps_m[:, 0:2 * ND], zero[:], zero[:, 0:2 * ND], start=True, stop=False)

                def tile(k, p, half):
                    pe.wait_ge(h_done, k + 1)
                    when(pe, hT_done, k - 1)
                    for c in range(ND):
                        last = pe.transpose(ps_t[p][:, c * P:(c + 1) * P], hb[:, p, c * P:(c + 1) * P], ident[:])
                    last.then_inc(tr_done, 1)
                    pe.wait_ge(v_in[p], 16 * half + 16)
                    for c in range(ND):
                        pe.matmul(ps_m[:, c:c + 1], hb[:, p, c * P:(c + 1) * P], share[:],
                                  start=False, stop=False, skip_group_check=True)
                    for c in range(ND):
                        last = pe.matmul(ps_m[:, ND + c:ND + c + 1], vb[:, p, c * P:(c + 1) * P], share[:],
                                         start=False, stop=False, skip_group_check=True)
                    last.then_inc(v_summed, 1)
                    pe.wait_ge(hT_done, k + 1)
                    when(pe, hp_copied, k - 1)
                    for c in range(ND):
                        pe.matmul(ps_h[p][:], hT[:, p, c * P:(c + 1) * P], wa[:, c, 0:D],
                                  start=c == 0, stop=c == ND - 1)
                    for c in range(ND):
                        last = pe.matmul(ps_f[p][:, 0:2 * H], hT[:, p, c * P:(c + 1) * P],
                                         wa[:, c, D:D + 2 * H], start=c == 0, stop=c == ND - 1)
                    last.then_inc(proj_done, 1)

                for p in range(2):
                    tile(p, p, 0)
                with pe.Fori(1, T // 2) as i:
                    for p in range(2):
                        tile(i * 2 + p, p, i)
                pe.matmul(ps_m[:, 0:2 * ND], zero[:], zero[:, 0:2 * ND], start=False, stop=True
                          ).then_inc(meanT_ps, 1)
                pe.wait_ge(meanT_done, 1)
                pe.wait_ge(hp_copied, T)
                for c in range(ND):
                    pe.matmul(ps_h[0][:], meanT[:, c:c + 1].to_broadcast((P, P)), wa[:, c, 0:D],
                              start=c == 0, stop=c == ND - 1)
                for c in range(ND):
                    last = pe.matmul(ps_b[:, c * P:(c + 1) * P], meanT[:, ND + c:ND + c + 1].to_broadcast((P, P)),
                                     ident[:], start=True, stop=True)
                last.then_inc(means_ps, 1)

        nc.clear_and_free_semaphores(mine)
        nc.all_engine_barrier()


def sort_rows(nc, records, before_in, degrees_in, row_index, tile_key, bank, f_src, found, flagged, n_flagged,
              g0, gkv):
    with ExitStack() as own:
        def sb(name, shape, dt=FP32):
            return own.enter_context(nc.sbuf_tensor(name, shape, dt))

        def sem(name):
            return own.enter_context(nc.semaphore(name))

        rec = sb("rec", [P, T, REC], I32)
        before = sb("before", [P, P], BF16)
        before_f = sb("before_f", [P, P])
        ones = sb("ones", [P, P], BF16)
        deg = sb("deg", [P, NDEG, T])
        keys = sb("keys", [P, T])
        row_of = sb("row_of", [P, T], I32)
        pad = sb("pad", [P, T, S])
        has = sb("has", [P, T, S])
        count = sb("count", [P, T])
        bad = sb("bad", [P, T], BF16)
        hot = sb("hot", [P, NDEG, T], BF16)
        total = sb("total", [P, NDEG * T])
        upto = sb("upto", [P, NDEG * T])
        nil = sb("nil", [P, NDEG * T])
        rank_f = sb("rank_f", [P, T])
        rank = sb("rank", [P, T], I32)
        fk = sb("fk", [P, 2, T])
        fl = sb("fl", [P, T])
        nf = sb("nf", [P, 1])
        ps_c, ps_n, ps_f = bank[0:2], bank[2:4], bank[4]
        HALF = NDEG * T // 2

        in_ = sem("sort_in")
        chain = sem("sort_chain")
        sets = sem("sort_sets")
        hot_done = sem("hot_done")
        counted = sem("counted")
        rank_done = sem("rank_done")
        scattered = sem("scattered")

        with nc.Block() as block:
            @block.sync
            def _(sp):
                sp.dma_start(before_f[:], before_in).then_inc(in_, 16)
                sp.dma_start(deg[:].rearrange("p a t -> p (a t)"),
                             degrees_in.to_broadcast((P, NDEG * T))).then_inc(in_, 16)
                sp.dma_start(keys[:], tile_key.to_broadcast((P, T))).then_inc(in_, 16)
                sp.dma_start(row_of[:], row_index).then_inc(in_, 16)

            @block.vector
            def _(dve):
                links = [0]

                def link(ins):
                    links[0] += 1
                    ins.then_inc(chain, 1)
                    dve.wait_ge(chain, links[0])

                dve.memset(ones[:], 1.0).then_inc(sets, 1)
                dve.memset(nil[:], 0.0).then_inc(sets, 1)
                dve.memset(rec[:, :, R_ROW + 1:R_FSRC], 0).then_inc(sets, 1)
                dve.tensor_copy(rec[:, :, R_FSRC:REC].bitcast(FP32), f_src[:])
                link(dve.tensor_scalar(has[:], found[:, :, 0:S], 0.0, None, ALU.is_gt))
                link(dve.reduce_sum(count[:], has[:], AX.X))
                dve.wait_ge(in_, 64)
                dve.tensor_copy(before[:], before_f[:])
                dve.tensor_copy(rec[:, :, R_ROW], row_of[:])
                dve.tensor_tensor(bad[:], count[:], found[:, :, S], ALU.not_equal)
                dve.tensor_tensor(hot[:], count[:, None, :].to_broadcast((P, NDEG, T)), deg[:], ALU.is_equal
                                  ).then_inc(hot_done, 1)
                dve.tensor_copy(rec[:, :, R_COUNT], count[:])
                link(dve.tensor_scalar(pad[:], found[:, :, 0:S], 0.0, float(NO_NODE + 1), ALU.is_equal, ALU.mult))
                link(dve.scalar_tensor_tensor(rec[:, :, 0:S], found[:, :, 0:S], -1.0, pad[:], ALU.add, ALU.add))
                dve.wait_ge(sets, 3)
                dve.wait_ge(counted, 1)
                for i in range(2):
                    last = dve.tensor_copy(total[:, i * HALF:(i + 1) * HALF], ps_n[i][:, 0:HALF])
                link(last)
                link(dve.tensor_tensor_scan(upto[:], total[:], nil[:], 0.0, ALU.add, ALU.add))
                link(dve.tensor_tensor(upto[:], upto[:], total[:], ALU.subtract))
                for i in range(2):
                    part = upto[:, i * HALF:(i + 1) * HALF]
                    last = dve.tensor_tensor(part, part, ps_c[i][:, 0:HALF], ALU.add)
                link(last)
                link(dve.tensor_tensor(upto[:], upto[:], hot[:].rearrange("p a t -> p (a t)"), ALU.mult))
                link(dve.reduce_sum(rank_f[:], upto[:].rearrange("p (a t) -> p t a", t=T), AX.X))
                dve.tensor_copy(rank[:], rank_f[:]).then_inc(rank_done, 1)
                link(dve.tensor_scalar(fl[:], ps_f[:, 0:T], 0.0, None, ALU.is_gt))
                link(dve.reduce_sum(nf[:], fl[:], AX.X))
                dve.tensor_copy(n_flagged[:], nf[0:1, :])
                link(dve.tensor_tensor(fk[:, 0, :], fl[:], keys[:], ALU.mult))
                for r in range(T // TOP):
                    link(dve.max(fl[:, r * TOP:(r + 1) * TOP], fk[:, r % 2, :]))
                    if r + 1 < T // TOP:
                        link(dve.match_replace(fk[:, (r + 1) % 2, :], fl[:, r * TOP:(r + 1) * TOP],
                                               fk[:, r % 2, :], 0.0))
                dve.tensor_scalar(flagged[:], fl[0:1, :], -1.0, 0.0, ALU.add, ALU.max)
                dve.memset(gkv[:, :, 0, :], 0.0)

            @block.scalar
            def _(act):
                act.wait_ge(sets, 2)
                act.activation(gkv[:, :, 1, :], nil[:, None, 0:D].to_broadcast((P, S + TWIN, D)), ACT.Copy)
                act.activation(g0[:], nil[:, None, 0:ROW].to_broadcast((P, S + TWIN, ROW)), ACT.Copy)

            @block.tensor
            def _(pe):
                pe.wait_ge(sets, 3)
                pe.wait_ge(hot_done, 1)
                flat = hot[:].rearrange("p a t -> p (a t)")
                for i in range(2):
                    pe.matmul(ps_c[i][:, 0:HALF], before[:], flat[:, i * HALF:(i + 1) * HALF], start=True, stop=True)
                    pe.matmul(ps_n[i][:, 0:HALF], ones[:], flat[:, i * HALF:(i + 1) * HALF], start=True, stop=True)
                pe.matmul(ps_f[:, 0:T], ones[:], bad[:], start=True, stop=True).then_inc(counted, 1)

            @block.gpsimd
            def _(pool):
                pool.wait_ge(rank_done, 1)
                for t in range(T):
                    pool.indirect_dma_start(records, bass.IndirectOffsetOnAxis(rank[:, t:t + 1], 0),
                                            rec[:, t, :], None).then_inc(scattered, 16)
                pool.wait_ge(scattered, 16 * T)


def sparse_layers(nc, x, kv, table, records, out, psum, ident, eps_c, found, mean_hp, mean_v, held, g0, gkv):
    with ExitStack() as own:
        def sb(name, shape, dt=FP32):
            return own.enter_context(nc.sbuf_tensor(name, shape, dt))

        def sem(name):
            return own.enter_context(nc.semaphore(name))

        NCH = len(CHUNKS)
        HALF_S = S // 2
        srt = sb("srt", [P, T, REC], I32)
        srt_f = srt[:, :, R_FSRC:REC].bitcast(FP32)
        fill = found[:, :, 0:S]
        some = found[:, :, S:S + 1]
        none = sb("none", [P, T, 1])
        idx0 = sb("idx0", [P, 2, S + 2], I32)
        idx1 = sb("idx1", [P, 2, S], I32)
        idx_out = sb("idx_out", [P, 2, 1], I32)
        xs = sb("xs", [P, 2, D])
        x1 = sb("x1", [P, 2, D])
        h1 = sb("h1", [P, 1, D])
        y = sb("y", [P, 2, D])
        em = sb("em", [P, D])
        sc = [sb(f"sc{layer}", [P, S, H]) for layer in range(2)]
        pr = [sb(f"pr{layer}", [P, S, H]) for layer in range(2)]
        al = [sb(f"al{layer}", [P, S, H]) for layer in range(2)]
        top = [sb(f"top{layer}", [P, H]) for layer in range(2)]
        den = [sb(f"den{layer}", [P, H]) for layer in range(2)]
        rden = [sb(f"rden{layer}", [P, H]) for layer in range(2)]
        nden = [sb(f"nden{layer}", [P, H]) for layer in range(2)]
        diag = sb("diag", [P, 2, P])
        st = sb("st3", [P, 6])
        mv = sb("mv3", [P, 2])
        negm = sb("negm3", [P, 1])
        lnv = sb("lnv3", [P, 1])
        rstd = sb("rstd3", [P, 1])
        nbias = sb("nbias3", [P, 1])
        acc0 = [psum[:, p, :] for p in range(2)]
        acc1 = [psum[:, 2 + p, :] for p in range(2)]
        PART = 2
        qk = [psum[:, 4 + PART * r:4 + PART * (r + 1), :] for r in range(2)]

        srt_in = sem("srt_in")
        cleared = sem("cleared")
        told = sem("told")
        sc_more = sem("sc_more")
        idx_done = sem("idx_done")
        idx1_done = sem("idx1_done")
        idx_out_done = sem("idx_out_done")
        xs_in = [sem(f"xs_in{p}") for p in range(2)]
        g0_in = [[sem(f"g0_in{c}_{p}") for p in range(2 if s0 < TWIN else 1)] for c, (s0, _) in enumerate(CHUNKS)]
        g0_weighted = [sem(f"g0_weighted{c}") for c in range(NCH)]
        g0_free = [sem(f"g0_free{c}") for c in range(NCH)]
        kv_in = [[sem(f"kv_in{c}_{p}") for p in range(2 if s0 < TWIN else 1)] for c, (s0, _) in enumerate(CHUNKS)]
        qk_done = [sem(f"qk_done{c}") for c in range(NCH)]
        v_weighted = [sem(f"v_weighted{c}") for c in range(NCH)]
        kv_free = [sem(f"kv_free{c}") for c in range(NCH)]
        soft = [sem(f"soft{layer}") for layer in range(2)]
        exp_done = [sem(f"exp_done{layer}") for layer in range(2)]
        LINKS = (10, 7)
        diag_done = sem("diag_done")
        acc0_done = sem("acc0_done")
        acc1_done = sem("acc1_done")
        neg_done = sem("neg_done")
        em_done = sem("em_done")
        fin = sem("fin")
        ln_chain = sem("ln_chain3")
        h1_done = sem("h1_done")
        y_done = sem("y_done")
        out_stored = [sem(f"out_stored{p}") for p in range(2)]

        def slots(engine, k):
            return engine.value_load(srt[0:1, k, R_COUNT:R_COUNT + 1], min_val=0, max_val=S)

        def over_chunks(engine, n, work, start=0, stop=S):
            with ExitStack() as nest:
                for c, (s0, m) in enumerate(CHUNKS):
                    if start <= s0 < stop:
                        if c:
                            nest.enter_context(engine.If(n > s0))
                        work(c, s0, m)

        def place(s, p):
            return s + p * TWIN if s < TWIN else s + TWIN

        def tiles(engine, step):
            for k in range(2):
                step(k, k, 0)
            with engine.Fori(1, T // 2 - 1) as i:
                for p in range(2):
                    step(i * 2 + p, p, i)
            step(T - 2, 0, T // 2 - 1, last=True)

        with nc.Block() as block:
            @block.sync
            def _(sp):
                sp.dma_start(srt[:], records.rearrange("(t p) r -> p t r", p=P)).then_inc(srt_in, 16)

            @block.gpsimd
            def _(pool):
                pool.wait_ge(srt_in, 16)

                def fetch0(k, p):
                    hold_when(pool, held["pool"], h1_done, k - 1)
                    pool.tensor_copy(idx0[:, p, :], srt[:, k, 0:S + 2]).then_inc(idx_done, 1)
                    n = slots(pool, k)
                    hold(pool, held["pool"], idx_done, k + 1)
                    pool.indirect_dma_start(xs[:, p, :], None, x,
                                            bass.IndirectOffsetOnAxis(idx0[:, p, R_ROW:R_ROW + 1], 0)
                                            ).then_inc(xs_in[p], 16)
                    def gather(c, s0, m):
                        hold_when(pool, held["pool"], g0_free[c], k - 1 if s0 < TWIN else k)
                        for s in range(s0, s0 + m):
                            pool.indirect_dma_start(g0[:, place(s, p), :], None, table,
                                                    bass.IndirectOffsetOnAxis(idx0[:, p, s:s + 1], 0),
                                                    bounds_check=N - 1, oob_is_err=False
                                                    ).then_inc(g0_in[c][p if s0 < TWIN else 0], 16)
                    over_chunks(pool, n, gather)

                def fetch1(k, p, n, **part):
                    def gather(c, s0, m):
                        hold_when(pool, held["pool"], kv_free[c], k - 1 if s0 < TWIN else k)
                        for s in range(s0, s0 + m):
                            pool.indirect_dma_start(
                                gkv[:, place(s, p), :, :].rearrange("p k d -> p (k d)"), None, kv,
                                bass.IndirectOffsetOnAxis(idx1[:, p, s:s + 1], 0),
                                bounds_check=N - 1, oob_is_err=False
                                ).then_inc(kv_in[c][p if s0 < TWIN else 0], 16)
                    over_chunks(pool, n, gather, **part)

                def first1(k, p):
                    pool.tensor_copy(idx1[:, p, :], srt[:, k, 0:S]).then_inc(idx1_done, 1)
                    hold(pool, held["pool"], idx1_done, k + 1)
                    fetch1(k, p, slots(pool, k), stop=TWIN)

                def rest1(k, p):
                    fetch1(k, p, slots(pool, k), start=TWIN)

                def store(k, p):
                    hold(pool, held["pool"], y_done, k + 1)
                    pool.tensor_copy(idx_out[:, p, :], srt[:, k, R_ROW:R_ROW + 1]).then_inc(idx_out_done, 1)
                    hold(pool, held["pool"], idx_out_done, k + 1)
                    pool.indirect_dma_start(out, bass.IndirectOffsetOnAxis(idx_out[:, p, :], 0),
                                            y[:, p, :], None).then_inc(out_stored[p], 16)

                def step(k, p, half, last=False):
                    rest1(k, p)
                    if not isinstance(k, int) or k:
                        store(k - 1, 1 - p)
                    first1(k + 1, 1 - p)
                    if not last:
                        fetch0(k + 2, p)

                fetch0(0, 0)
                first1(0, 0)
                fetch0(1, 1)
                tiles(pool, step)
                rest1(T - 1, 1)
                store(T - 2, 0)
                store(T - 1, 1)
                for p in range(2):
                    pool.wait_ge(out_stored[p], 16 * T // 2)

            @block.vector
            def _(dve):
                for layer in range(2):
                    dve.memset(sc[layer][:], 0.0).then_inc(cleared, 1)
                dve.wait_ge(cleared, 2)
                hold(dve, held["dve"], srt_in, 16)
                dve.tensor_scalar(fill, srt[:, :, 0:S], float(N), NEG_FILL, ALU.is_ge, ALU.mult).then_inc(told, 1)
                dve.tensor_scalar(some, srt[:, :, R_COUNT:R_COUNT + 1], 0.0, None, ALU.is_gt).then_inc(told, 1)
                dve.tensor_scalar(none[:], srt[:, :, R_COUNT:R_COUNT + 1], 0.0, None, ALU.is_equal
                                  ).then_inc(told, 1)
                dve.wait_ge(told, 3)

                def of(t, k):
                    return t[:, k:k + 1] if isinstance(k, int) else t[:, bass.ds(k, 1)]

                def by_head(t):
                    return t[:].rearrange("p s h -> p h s")

                def over_slots(t):
                    return t[:, None, :].to_broadcast((P, S, H))

                def query_keys(k, p, half, n):
                    dve.wait_ge(h1_done, k + 1)
                    def work(c, s0, m):
                        parts = m // PART
                        first = sum(SLOT_COUNTS[:c]) // PART
                        if s0 < TWIN:
                            dve.wait_ge(kv_in[c][p], (half + 1) * (16 * m))
                        else:
                            dve.wait_ge(kv_in[c][0], (k + 1) * (16 * m))
                        for r in range(parts):
                            at = place(s0 + r * PART, p)
                            dve.tensor_tensor(qk[(first + r) % 2], gkv[:, at:at + PART, 0, :],
                                              h1[:].to_broadcast((P, PART, D)), ALU.mult).then_inc(qk_done[c], 1)
                        for r in range(parts):
                            dve.wait_ge(qk_done[c], k * (2 * parts) + r + 1)
                            dve.tensor_reduce(sc[1][:, s0 + r * PART:s0 + (r + 1) * PART, :],
                                              qk[(first + r) % 2].rearrange("p s (h f) -> p s h f", h=H),
                                              AX.X, ALU.add).then_inc(qk_done[c], 1)
                        hold(dve, held["dve"], qk_done[c], (k + 1) * (2 * parts))
                    over_chunks(dve, n, work)

                def prepare(k, p, n, half):
                    def work(c, s0, m):
                        if s0 < TWIN:
                            hold(dve, held["dve"], g0_in[c][p], (half + 1) * (16 * m))
                        else:
                            hold(dve, held["dve"], g0_in[c][0], (k + 1) * (16 * m))
                    over_chunks(dve, n, work, stop=HALF_S)
                    for a, b in ((0, TWIN), (TWIN, HALF_S)):
                        dve.tensor_tensor(sc[0][:, a:b, :], g0[:, place(a, p):place(b - 1, p) + 1, D:ROW],
                                          of(srt_f, k).to_broadcast((P, b - a, H)), ALU.add).then_inc(soft[0], 1)
                    with dve.If(n > HALF_S):
                        def work(c, s0, m):
                            hold(dve, held["dve"], g0_in[c][0], (k + 1) * (16 * m))
                        over_chunks(dve, n, work, start=HALF_S)
                        dve.tensor_tensor(sc[0][:, HALF_S:S, :], g0[:, place(HALF_S, p):place(S - 1, p) + 1, D:ROW],
                                          of(srt_f, k).to_broadcast((P, S - HALF_S, H)), ALU.add
                                          ).then_inc(sc_more, 1)
                        hold(dve, held["dve"], sc_more, k + 1)
                    dve.wait_ge(soft[0], k * LINKS[0] + 2)
                    dve.scalar_tensor_tensor(sc[0][:], sc[0][:], ALPHA, sc[0][:], ALU.mult, ALU.max
                                             ).then_inc(soft[0], 1)
                    dve.wait_ge(soft[0], k * LINKS[0] + 3)

                def shift(layer, k, at):
                    dve.tensor_tensor(sc[layer][:], sc[layer][:],
                                      of(fill, k).rearrange("p o s -> p s o").to_broadcast((P, S, H)), ALU.add
                                      ).then_inc(soft[layer], 1)
                    dve.wait_ge(soft[layer], k * LINKS[layer] + at + 1)
                    dve.reduce_max(top[layer][:], by_head(sc[layer]), AX.X).then_inc(soft[layer], 1)
                    dve.wait_ge(soft[layer], k * LINKS[layer] + at + 2)
                    dve.tensor_tensor(sc[layer][:], sc[layer][:], over_slots(top[layer]), ALU.subtract
                                      ).then_inc(soft[layer], 1)

                def attention(layer, k, at):
                    dve.wait_ge(exp_done[layer], k + 1)
                    dve.reduce_sum(den[layer][:], by_head(pr[layer]), AX.X).then_inc(soft[layer], 1)
                    dve.wait_ge(soft[layer], k * LINKS[layer] + at + 1)
                    dve.reciprocal(rden[layer][:], den[layer][:]).then_inc(soft[layer], 1)
                    dve.wait_ge(soft[layer], k * LINKS[layer] + at + 2)
                    dve.tensor_scalar(nden[layer][:], rden[layer][:], some[:, k, :], None, ALU.mult
                                      ).then_inc(soft[layer], 1)
                    dve.wait_ge(soft[layer], k * LINKS[layer] + at + 3)
                    dve.tensor_tensor(al[layer][:], pr[layer][:], over_slots(nden[layer]), ALU.mult
                                      ).then_inc(soft[layer], 1)
                    dve.wait_ge(soft[layer], k * LINKS[layer] + at + 4)

                def weigh(layer, k, p, n):
                    def work(c, s0, m):
                        at = place(s0, p)
                        rows = g0[:, at:at + m, 0:D] if layer == 0 else gkv[:, at:at + m, 1, :]
                        rows = rows.rearrange("p s (h f) -> p s h f", h=H)
                        dve.tensor_tensor(rows, rows,
                                          al[layer][:, s0:s0 + m, :, None].to_broadcast((P, m, H, F)),
                                          ALU.mult).then_inc((g0_weighted, v_weighted)[layer][c], 1)
                    over_chunks(dve, n, work)

                def finish0(k, p, half):
                    dve.wait_ge(em_done, k + 1)
                    when(dve, acc1_done, k - 1)
                    dve.scalar_tensor_tensor(x1[:, p, :], acc0[p], 0.0, em[:], ALU.max, ALU.add).then_inc(fin, 1)
                    dve.wait_ge(xs_in[p], 16 * half + 16)
                    dve.wait_ge(fin, k * 5 + 1)
                    dve.scalar_tensor_tensor(x1[:, p, :], x1[:, p, :], -1.0, xs[:, p, :], ALU.add, ALU.add
                                             ).then_inc(fin, 1)
                    dve.wait_ge(fin, k * 5 + 2)
                    dve.bn_stats(st[:], x1[:, p, :]).then_inc(fin, 1)
                    hold(dve, held["dve"], fin, k * 5 + 3)
                    dve.bn_aggr(mv[:], st[:]).then_inc(fin, 1)
                    dve.wait_ge(fin, k * 5 + 4)
                    dve.tensor_scalar(negm[:], mv[:, 0:1], -1.0, None, ALU.mult).then_inc(fin, 1)

                def layer0(k, p, half):
                    n = slots(dve, k)
                    prepare(k, p, n, half)
                    shift(0, k, 3)
                    attention(0, k, 6)
                    weigh(0, k, p, n)

                def layer1(k, p, half, beside=None):
                    n = slots(dve, k)
                    query_keys(k, p, half, n)
                    shift(1, k, 0)
                    if beside:
                        beside()
                    attention(1, k, 3)
                    weigh(1, k, p, n)

                def step(k, p, half, last=False):
                    layer1(k, p, half, lambda: finish0(k + 1, 1 - p, half + p))
                    if not last:
                        layer0(k + 2, p, half + 1)

                layer0(0, 0, 0)
                finish0(0, 0, 0)
                layer0(1, 1, 0)
                tiles(dve, step)
                layer1(T - 1, 1, T // 2 - 1)

            @block.scalar
            def _(act):
                act.wait_ge(told, 3)

                def exponentials(layer, k):
                    act.wait_ge(soft[layer], k * LINKS[layer] + (6, 3)[layer])
                    act.activation(pr[layer][:], sc[layer][:], ACT.Exp, scale=(1.0, SCALE)[layer]
                                   ).then_inc(exp_done[layer], 1)

                def negative_part(k, p):
                    act.wait_ge(acc0_done, k + 1)
                    act.activation(em[:], acc0[p], ACT.Relu, scale=-1.0).then_inc(neg_done, 1)
                    act.wait_ge(neg_done, k + 1)
                    act.activation(em[:], em[:], ACT.Exp, scale=-1.0).then_inc(em_done, 1)

                def normalise(k, p):
                    act.wait_ge(fin, k * 5 + 5)
                    act.activation(lnv[:], mv[:, 1:2], ACT.Ln, bias=eps_c[:]).then_inc(ln_chain, 1)
                    act.wait_ge(ln_chain, k * 3 + 1)
                    act.activation(rstd[:], lnv[:], ACT.Exp, scale=-0.5).then_inc(ln_chain, 1)
                    act.wait_ge(ln_chain, k * 3 + 2)
                    act.activation(nbias[:], negm[:], ACT.Copy, scale=rstd[:]).then_inc(ln_chain, 1)
                    act.wait_ge(ln_chain, k * 3 + 3)
                    act.activation(h1[:, 0, :], x1[:, p, :], ACT.Relu, bias=nbias[:], scale=rstd[:]
                                   ).then_inc(h1_done, 1)

                def diagonal(k, p):
                    act.activation(diag[:, p, :], ident[:], ACT.Copy, scale=none[:, k, :]).then_inc(diag_done, 1)

                def output(k, p, half):
                    act.wait_ge(acc1_done, k + 1)
                    when(act, out_stored[p], 16 * half)
                    act.activation(y[:, p, :], acc1[p], ACT.Copy).then_inc(y_done, 1)

                def step(k, p, half, last=False):
                    negative_part(k + 1, 1 - p)
                    exponentials(1, k)
                    normalise(k + 1, 1 - p)
                    if not last:
                        exponentials(0, k + 2)
                    output(k, p, half)
                    if not last:
                        diagonal(k + 2, p)

                exponentials(0, 0)
                diagonal(0, 0)
                negative_part(0, 0)
                normalise(0, 0)
                exponentials(0, 1)
                diagonal(1, 1)
                tiles(act, step)
                exponentials(1, T - 1)
                output(T - 1, 1, T // 2 - 1)

            @block.tensor
            def _(pe):
                pe.wait_ge(srt_in, 16)

                def add_up(k, n, acc, weighted, free, rows):
                    def add(c, s0, m):
                        pe.wait_ge(weighted[c], k + 1)
                        for s in range(s0, s0 + m):
                            last = pe.matmul(acc, ident[:], rows(s), start=s == 0, stop=False)
                        last.then_inc(free[c], 1)
                    over_chunks(pe, n, add)

                def layer0(k, p, n):
                    when(pe, fin, k * 5 - 9)
                    add_up(k, n, acc0[p], g0_weighted, g0_free, lambda s: g0[:, place(s, p), 0:D])
                    pe.wait_ge(diag_done, k + 1)
                    pe.matmul(acc0[p], diag[:, p, :], mean_hp[:], start=False, stop=True
                              ).then_inc(acc0_done, 1)

                def layer1(k, p, n):
                    when(pe, y_done, k - 1)
                    add_up(k, n, acc1[p], v_weighted, kv_free, lambda s: gkv[:, place(s, p), 1, :])
                    pe.matmul(acc1[p], diag[:, p, :], mean_v[:], start=False, stop=False)
                    pe.matmul(acc1[p], ident[:], x1[:, p, :], start=False, stop=True).then_inc(acc1_done, 1)

                def step(k, p, half, last=False):
                    layer1(k, p, slots(pe, k))
                    if not last:
                        layer0(k + 2, p, slots(pe, k + 2))

                for p in range(2):
                    layer0(p, p, slots(pe, p))
                tiles(pe, step)
                layer1(T - 1, 1, slots(pe, T - 1))


def dense_layers(nc, x_t, adj_t, table_t, kv_t, out_t, bank, ident, eps_c, f_src, held, flagged, n_flagged):
    ctx = ExitStack()
    with ctx:
        def sb(name, shape, dt=FP32):
            return ctx.enter_context(nc.sbuf_tensor(name, shape, dt))

        def sem(name):
            return ctx.enter_context(nc.semaphore(name))

        hp = sb("g_hp", [P, T, ROW])
        kvh = sb("g_kvh", [P, T, 2, F])
        val = sb("g_val", [P, T, F])
        fdc = sb("g_fdc", [P, T])
        fill = sb("g_fill", [P, N])
        adj_b = fill[:].bitcast(I32)
        e = sb("g_e", [P, N])
        pT = sb("g_pT", [P, N])
        kT = pT
        x0 = sb("g_x0", [P, D])
        o = sb("g_o", [P, D])
        t0 = sb("g_t0", [P, D])
        t0n = sb("g_t0n", [P, D])
        t0e = sb("g_t0e", [P, D])
        h1 = sb("g_h1", [P, D])
        q = sb("g_q", [P, F])
        qT = sb("g_qT", [F, P])
        st = sb("g_st", [P, 6])
        mv = sb("g_mv", [P, 2])
        lnv = sb("g_lnv", [P, 1])
        rstd = sb("g_rstd", [P, 1])
        nb = sb("g_nb", [P, 1])
        nm = sb("g_nm", [P, 1])
        den = sb("g_den", [P, 1])
        rden = sb("g_rden", [P, 1])
        ps_e, ps_t, ps_o = bank[0:2], bank[2:4], bank[4]
        ps_q = bank[5]

        table_in = sem("g_table_in")
        xa_in = sem("g_xa_in")
        fill_done = sem("g_fill_done")
        row = sem("g_row")
        tile_done = sem("g_tile_done")
        out_stored = sem("g_out_stored")
        elu_neg = sem("g_elu_neg")
        elu_exp = sem("g_elu_exp")
        acc0 = sem("g_acc0")
        x1_done = sem("g_x1_done")
        stats = sem("g_stats")
        lnd = sem("g_lnd")
        rstd_done = sem("g_rstd_done")
        nb_done = sem("g_nb_done")
        h1_done = sem("g_h1_done")

        names = ("head", "kv_in", "kT_ps", "kT", "qT_ps", "qT", "block", "read", "leaky", "masked",
                 "top", "shift", "exp", "pT_ps", "pT", "weighted", "rden", "out")
        s0, s1 = [{n: sem(f"g{layer}_{n}") for n in names} for layer in range(2)]

        with nc.Block() as block:
            @block.sync
            def _(sp):
                sp.sem_inc(out_stored, 1)
                n = sp.value_load(n_flagged[:], min_val=0, max_val=T)
                with sp.If(n > 0):
                    sp.dma_start(hp[:], table_t).then_inc(table_in, 16)
                    with sp.Fori(0, n) as g:
                        t = sp.value_load(flagged[0:1, bass.ds(g, 1)], min_val=0, max_val=T - 1)
                        sp.wait_ge(tile_done, g + 1)
                        sp.dma_start(x0[:], x_t[:, t, :]).then_inc(xa_in, 16)
                        sp.dma_start(adj_b, adj_t[:, t, :]).then_inc(xa_in, 16)
                        with sp.Fori(0, H) as h:
                            sp.wait_ge(s1["weighted"], g * H + h + 1)
                            for k in range(2):
                                sp.dma_start(kvh[:, :, k, :], kv_t[:, :, k, h, :]).then_inc(s1["kv_in"], 16)
                        sp.wait_ge(tile_done, g + 2)
                        sp.dma_start(out_t[:, t, :], t0[:]).then_inc(out_stored, 16)
                    hold(sp, held["sp"], out_stored, n * 16 + 1)

            @block.vector
            def _(dve):
                dve.sem_inc(tile_done, 1)
                dve.sem_inc(s0["out"], 1)
                dve.sem_inc(s1["out"], 1)
                def attend(s, u, h):
                    dve.scalar_tensor_tensor(e[:], fill[:], NEG_FILL, e[:], ALU.add, ALU.min
                                             ).then_inc(s["masked"], 1)
                    dve.wait_ge(s["masked"], u + 1)
                    dve.reduce_max(nm[:], e[:], AX.X).then_inc(s["top"], 1)
                    dve.wait_ge(s["top"], u + 1)
                    dve.tensor_scalar(nm[:], nm[:], -1.0 if s is s0 else -SCALE, None, ALU.mult
                                      ).then_inc(s["shift"], 1)
                    dve.wait_ge(s["exp"], u + 1)
                    dve.reciprocal(rden[:], den[:]).then_inc(s["rden"], 1)
                    dve.wait_ge(s["rden"], u + 1)
                    dve.wait_ge(s["weighted"], u + 2)
                    dve.tensor_scalar(o[:, bass.ds(h * F, F)], ps_o[:, 0:F], rden[:], None, ALU.mult
                                      ).then_inc(s["out"], 1)

                n = dve.value_load(n_flagged[:], min_val=0, max_val=T)
                with dve.If(n > 0):
                    dve.wait_ge(table_in, 16)
                    with dve.Fori(0, n) as g:
                        t = dve.value_load(flagged[0:1, bass.ds(g, 1)], min_val=0, max_val=T - 1)
                        dve.wait_ge(xa_in, g * 32 + 32)
                        dve.tensor_scalar(fill[:], adj_b, 0.0, BIG, ALU.is_gt, ALU.mult).then_inc(fill_done, 1)
                        with dve.Fori(0, H) as h:
                            u = g * H + h
                            dve.wait_ge(s0["weighted"], u + 1)
                            dve.tensor_copy(val[:], hp[:, :, bass.ds(h * F, F)]).then_inc(s0["head"], 1)
                            dve.tensor_copy(fdc[:], hp[:, :, bass.ds(h + D, 1)].rearrange("p t o -> p (t o)")
                                            ).then_inc(s0["head"], 1)
                            for b in range(NB):
                                dve.wait_ge(s0["block"], u * NB + b + 1)
                                dve.tensor_scalar(e[:, b * BLK:(b + 1) * BLK], ps_e[b % 2][:],
                                                  f_src[:, t, bass.ds(h, 1)], None, ALU.add
                                                  ).then_inc(s0["read"], 1)
                            dve.wait_ge(s0["read"], u * NB + NB + 2)
                            dve.scalar_tensor_tensor(e[:], e[:], ALPHA, e[:], ALU.mult, ALU.max
                                                     ).then_inc(s0["leaky"], 1)
                            dve.wait_ge(s0["leaky"], u + 1)
                            dve.wait_ge(fill_done, g + 1)
                            attend(s0, u, h)
                        dve.wait_ge(elu_exp, g + 1)
                        dve.wait_ge(out_stored, g * 16 + 1)
                        dve.scalar_tensor_tensor(t0[:], o[:], 0.0, t0e[:], ALU.max, ALU.add).then_inc(acc0, 1)
                        dve.wait_ge(acc0, g + 1)
                        dve.scalar_tensor_tensor(x0[:], t0[:], -1.0, x0[:], ALU.add, ALU.add).then_inc(x1_done, 1)
                        dve.wait_ge(x1_done, g + 1)
                        dve.bn_stats(st[:], x0[:]).then_inc(stats, 1)
                        hold(dve, held["dve"], stats, 2 * g + 1)
                        dve.bn_aggr(mv[:], st[:]).then_inc(stats, 1)
                        dve.wait_ge(stats, 2 * g + 2)
                        dve.wait_ge(rstd_done, g + 1)
                        dve.tensor_scalar(nb[:], mv[:, 0:1], rstd[:], -1.0, ALU.mult, ALU.mult).then_inc(nb_done, 1)
                        hold(dve, held["dve"], h1_done, g + 1)
                        with dve.Fori(0, H) as h:
                            u = g * H + h
                            dve.wait_ge(s1["weighted"], u + 1)
                            dve.tensor_copy(q[:], h1[:, bass.ds(h * F, F)]).then_inc(s1["head"], 1)
                            for b in range(NB):
                                dve.wait_ge(s1["block"], u * NB + b + 1)
                                dve.tensor_copy(e[:, b * BLK:(b + 1) * BLK], ps_e[b % 2][:]).then_inc(s1["read"], 1)
                            dve.wait_ge(s1["read"], u * NB + NB + 2)
                            attend(s1, u, h)
                        dve.wait_ge(s1["out"], (g + 1) * H + 1)
                        dve.tensor_tensor(t0[:], o[:], x0[:], ALU.add).then_inc(tile_done, 1)

            @block.scalar
            def _(act):
                def attend(s, u):
                    act.wait_ge(s["shift"], u + 1)
                    act.activation(e[:], e[:], ACT.Exp, bias=nm[:], scale=1.0 if s is s0 else SCALE,
                                   accum_out=den[:]).then_inc(s["exp"], 1)
                    for b in range(NB):
                        act.wait_ge(s["pT_ps"], u * NB + b + 1)
                        act.activation(pT[:, b * BLK:(b + 1) * BLK], ps_t[b % 2][:], ACT.Copy
                                       ).then_inc(s["pT"], 1)

                for s in (s0, s1):
                    act.sem_inc(s["pT"], 2)
                act.sem_inc(s1["kT"], 2)
                n = act.value_load(n_flagged[:], min_val=0, max_val=T)
                with act.If(n > 0):
                    with act.Fori(0, n) as g:
                        with act.Fori(0, H) as h:
                            attend(s0, g * H + h)
                        act.wait_ge(s0["out"], (g + 1) * H + 1)
                        act.activation(t0n[:], o[:], ACT.Relu, scale=-1.0).then_inc(elu_neg, 1)
                        act.wait_ge(elu_neg, g + 1)
                        act.activation(t0e[:], t0n[:], ACT.Exp, scale=-1.0).then_inc(elu_exp, 1)
                        act.wait_ge(stats, 2 * g + 2)
                        act.activation(lnv[:], mv[:, 1:2], ACT.Ln, bias=eps_c[:]).then_inc(lnd, 1)
                        act.wait_ge(lnd, g + 1)
                        act.activation(rstd[:], lnv[:], ACT.Exp, scale=-0.5).then_inc(rstd_done, 1)
                        act.wait_ge(nb_done, g + 1)
                        act.activation(h1[:], x0[:], ACT.Relu, bias=nb[:], scale=rstd[:]).then_inc(h1_done, 1)
                        with act.Fori(0, H) as h:
                            u = g * H + h
                            act.wait_ge(s1["qT_ps"], u + 1)
                            act.activation(qT[:], ps_q[0:F, 0:P], ACT.Copy).then_inc(s1["qT"], 1)
                            for b in range(NB):
                                act.wait_ge(s1["kT_ps"], u * NB + b + 1)
                                act.activation(kT[0:F, b * BLK:(b + 1) * BLK], ps_t[b % 2][0:F, :], ACT.Copy
                                               ).then_inc(s1["kT"], 1)
                            attend(s1, u)

            @block.tensor
            def _(pe):
                PB = BLK // P
                for s in (s0, s1):
                    pe.sem_inc(s["weighted"], 1)

                def attend(s, u, values):
                    pe.wait_ge(s["exp"], u + 1)
                    for b in range(NB):
                        pe.wait_ge(s["pT"], u * NB + b + 1)
                        for c in range(PB):
                            j = b * PB + c
                            last = pe.transpose(ps_t[b % 2][:, c * P:(c + 1) * P], e[:, j * P:(j + 1) * P], ident[:])
                        last.then_inc(s["pT_ps"], 1)
                    pe.wait_ge(s["pT"], u * NB + NB + 2)
                    pe.wait_ge(s["out"], u + 1)
                    for j in range(T):
                        last = pe.matmul(ps_o[:, 0:F], pT[:, j * P:(j + 1) * P], values(j),
                                         start=j == 0, stop=j == T - 1)
                    last.then_inc(s["weighted"], 1)

                n = pe.value_load(n_flagged[:], min_val=0, max_val=T)
                with pe.If(n > 0):
                    pe.wait_ge(table_in, 16)
                    with pe.Fori(0, n) as g:
                        with pe.Fori(0, H) as h:
                            u = g * H + h
                            pe.wait_ge(s0["head"], 2 * u + 2)
                            for b in range(NB):
                                pe.wait_ge(s0["read"], u * NB + b + 1)
                                for c in range(PB):
                                    j = b * PB + c
                                    last = pe.matmul(ps_e[b % 2][:, c * P:(c + 1) * P],
                                                     fdc[:, j:j + 1].to_broadcast((P, P)), ident[:],
                                                     start=True, stop=True)
                                last.then_inc(s0["block"], 1)
                            attend(s0, u, lambda j: val[:, j, :])
                        with pe.Fori(0, H) as h:
                            u = g * H + h
                            hold(pe, held["pe"], s1["head"], u + 1)
                            pe.transpose(ps_q[0:F, 0:P], q[:], ident[:]).then_inc(s1["qT_ps"], 1)
                            pe.wait_ge(s1["kv_in"], 32 * u + 32)
                            for b in range(NB):
                                hold(pe, held["pe"], s1["kT"], u * NB + b + 1)
                                for c in range(PB):
                                    j = b * PB + c
                                    last = pe.transpose(ps_t[b % 2][0:F, c * P:(c + 1) * P], kvh[:, j, 0, :], ident[:])
                                last.then_inc(s1["kT_ps"], 1)
                            pe.wait_ge(s1["qT"], u + 1)
                            for b in range(NB):
                                pe.wait_ge(s1["kT"], u * NB + b + 3)
                                pe.wait_ge(s1["read"], u * NB + b + 1)
                                pe.matmul(ps_e[b % 2][:], qT[:], kT[0:F, b * BLK:(b + 1) * BLK],
                                          start=True, stop=True).then_inc(s1["block"], 1)
                            attend(s1, u, lambda j: kvh[:, j, 1, :])

            @block.gpsimd
            def _(pool):
                pool.sem_inc(s0["read"], 2)
                pool.sem_inc(s1["read"], 2)


def kernel(x, adj, L0_gnn_W, L0_gnn_a, L1_gnn_x2, L1_gnn_v):
    import numpy as np
    import concourse.bacc as bacc
    from concourse.bass_utils import run_bass_kernel_spmd

    arrays = {
        "x": np.ascontiguousarray(x),
        "adj": np.ascontiguousarray(adj),
        "kv": np.concatenate([L1_gnn_x2, L1_gnn_v], axis=1),
        "w": np.ascontiguousarray(np.transpose(L0_gnn_W, (1, 0, 2)).reshape(D, D)),
        "a": np.ascontiguousarray(L0_gnn_a),
        "eye": np.eye(P, dtype=np.float32),
        "before": np.triu(np.ones((P, P), np.float32), 1),
        "seg_base": np.tile(np.repeat(np.arange(NS, dtype=np.float32) * SEG + 1, TOP), (P, 1)),
        "degrees": np.repeat(np.arange(S, -1, -1, dtype=np.float32), T)[None],
        "row_index": np.arange(N, dtype=np.int32).reshape(T, P).T.copy(),
        "tile_key": np.arange(1, T + 1, dtype=np.float32)[None],
    }
    nc = bacc.Bacc("TRN2", target_bir_lowering=False, num_devices=1)
    args = {n: nc.dram_tensor(f"in_{n}", v.shape, mybir.dt.from_np(v.dtype), kind="ExternalInput").ap()
            for n, v in arrays.items()}
    out = nc.dram_tensor("out", (N, D), FP32, kind="ExternalOutput").ap()
    graph_layers(nc, **args, out=out)
    r = run_bass_kernel_spmd(nc, [{f"in_{n}": v for n, v in arrays.items()}], core_ids=[0])
    return r.results[0]["out"]
```

```python
from contextlib import ExitStack

import concourse.bass as bass
from concourse import mybir

FP32 = mybir.dt.float32
BF16 = mybir.dt.bfloat16
I32 = mybir.dt.int32
U32 = mybir.dt.uint32
ALU = mybir.AluOpType
ACT = mybir.ActivationFunctionType
AX = mybir.AxisListType

P = 128
N = 4096
D = 512
H = 8
F = D // H
T = N // P
ROW = D + H
BLK = 512
NB = N // BLK
SCALE = float(F) ** -0.5
ALPHA = 0.2
EPS = 1e-5
BIG = 3.0e38
SEG = 512
NS = N // SEG
TOP = 8
S = 24
SLOT_COUNTS = (4, 2, 2, 2, 2, 2, 2, 4, 2, 2)
CHUNKS = [(sum(SLOT_COUNTS[:c]), m) for c, m in enumerate(SLOT_COUNTS)]
TWIN = 4
AIDED = (3, 2)
LN_EXP_SET = 6
NO_NODE = 2 * N
REC = 36
R_COUNT, R_ROW, R_FSRC = S, S + 1, S + 4
NDEG = S + 1
NEG_FILL = -9.0e15


def hold(engine, tally, sem, value):
    engine.wait_ge(sem, value)
    engine.sem_inc(tally, 1)


def load_exp_and_ln(nc, act):
    act.add_instruction(mybir.InstLoadActFuncSet(act_func_set_id=LN_EXP_SET, name=nc.get_next_instruction_name(),
                                                 engine=act.engine))


def when(engine, sem, value):
    if not isinstance(value, int) or value > 0:
        engine.wait_ge(sem, value)


def hold_when(engine, tally, sem, value):
    if not isinstance(value, int) or value > 0:
        hold(engine, tally, sem, value)


def graph_layers(nc, x, adj, kv, w, a, eye, before, seg_base, degrees, row_index, tile_key, out):
    table = nc.dram_tensor("projected", (N, ROW), FP32).ap()
    records = nc.dram_tensor("records", (N, REC), I32).ap()
    x_t = x.rearrange("(t p) d -> p t d", p=P)
    out_t = out.rearrange("(t p) d -> p t d", p=P)
    adj_t = adj.rearrange("(t p) n -> p t n", p=P)
    table_t = table.rearrange("(t p) d -> p t d", p=P)
    kv_t = kv.rearrange("(t p) (k h f) -> p t k h f", p=P, k=2, h=H)
    v_t = kv.rearrange("(t p) (k d) -> p t k d", p=P, k=2)

    ctx = ExitStack()
    with ctx:
        def sb(name, shape, dt=FP32):
            return ctx.enter_context(nc.sbuf_tensor(name, shape, dt))

        def sem(name):
            return ctx.enter_context(nc.semaphore(name))

        psum = ctx.enter_context(nc.psum_tensor("psum", [P, 8, BLK], FP32))
        bank = [psum[:, i, :] for i in range(8)]
        ident = sb("ident", [P, P])
        eps_c = sb("eps_c", [P, 1])
        f_src = sb("f_src", [P, T, H])
        found = sb("found", [P, T, S + 1])
        mean_hp = sb("mean_hp", [P, D])
        mean_v = sb("mean_v", [P, D])
        flagged = sb("flagged", [1, T], I32)
        n_flagged = sb("n_flagged", [1, 1], I32)
        held = {e: sem(f"held_{e}") for e in ("pe", "dve", "pool", "sp")}

        project_and_scan(nc, x_t, adj_t, table_t, w, a, eye, seg_base, bank, ident, eps_c, f_src,
                         found, mean_hp, held)
        with ExitStack() as slots:
            g0 = slots.enter_context(nc.sbuf_tensor("g0", [P, S + TWIN, ROW], FP32))
            gkv = slots.enter_context(nc.sbuf_tensor("gkv", [P, S + TWIN, 2, D], FP32))
            sort_rows(nc, v_t, records, before, degrees, row_index, tile_key, bank, f_src, found, mean_v,
                      flagged, n_flagged, g0, gkv)
            sparse_layers(nc, x, kv, table, records, out, psum, ident, eps_c, found, mean_hp, mean_v, held,
                          g0, gkv)
        dense_layers(nc, x_t, adj_t, table_t, kv_t, out_t, bank, ident, eps_c, f_src, held, flagged, n_flagged)


def project_and_scan(nc, x_t, adj_t, table_t, w, a, eye, seg_base_in, bank, ident, eps_c, f_src,
                     found, mean_hp, held):
    with ExitStack() as own:
        def sb(name, shape, dt=FP32):
            return own.enter_context(nc.sbuf_tensor(name, shape, dt))

        mine = []

        def sem(name):
            mine.append(nc.alloc_semaphore(name))
            return mine[-1]

        ND = D // P
        wa = sb("wa", [P, ND, D + 2 * H])
        a_bc = sb("a_bc", [P, H, 2, F])
        wprod = sb("wprod", [P, D])
        xb = sb("xb", [P, 2, D])
        hb = sb("hb", [P, 2, D])
        hT = sb("hT", [P, 2, D])
        rowb = sb("rowb", [P, 2, ROW])
        st = sb("st", [P, 2, 6])
        mv = sb("mv", [P, 2, 2])
        negm = sb("negm", [P, 2, 1])
        lnv = sb("lnv", [P, 2, 1])
        rstd = sb("rstd", [P, 2, 1])
        nbias = sb("nbias", [P, 2, 1])
        adjb = sb("adjb", [P, 2, N], I32)
        mask = sb("mask", [P, 2, NS, SEG + TOP], BF16)
        ones8 = sb("ones8", [P, TOP], BF16)
        nth = sb("nth", [P, 2, NS * TOP], U32)
        base = sb("base", [P, NS * TOP])
        key = sb("key", [P, 2, NS * TOP])
        rest = sb("rest", [P, 2, NS * TOP])
        first = sb("first", [P, 2, S])
        share = sb("share", [P, 1])
        zero = sb("zero", [P, P])
        meanT = sb("meanT", [P, ND])
        ps_t, ps_h, ps_f = bank[0:2], bank[2:4], bank[4:6]
        ps_m = bank[6]

        consts_in = sem("consts_in")
        x_in = [sem(f"x_in{p}") for p in range(2)]
        adj_in = [sem(f"adj_in{p}") for p in range(2)]
        sets = sem("sets")
        wprod_done = sem("wprod_done")
        wa_done = sem("wa_done")
        stats = sem("stats")
        ln_chain = sem("ln_chain")
        h_done = sem("h_done")
        tr_done = sem("tr_done")
        hT_done = sem("hT_done")
        proj_done = sem("proj_done")
        hp_copied = sem("hp_copied")
        mask_done = sem("mask_done")
        scanned = sem("scanned")
        compact = sem("compact")
        first_kept = sem("first_kept")
        meanT_ps = sem("meanT_ps")
        meanT_done = sem("meanT_done")
        mean_ps = sem("mean_ps")
        stored = [sem(f"stored{p}") for p in range(2)]
        NCONST = 4
        LINKS = 2 + 2 * S // TOP - 1

        with nc.Block() as block:
            @block.sync
            def _(sp):
                sp.dma_start(ident[:], eye).then_inc(consts_in, 16)
                sp.dma_start(base[:], seg_base_in).then_inc(consts_in, 16)
                sp.dma_start(wa[:, :, 0:D], w.rearrange("(c p) n -> p c n", p=P)).then_inc(consts_in, 16)
                sp.dma_start(a_bc[:].rearrange("p h s f -> p (h s f)"),
                             a.rearrange("(o h) f -> o (h f)", o=1).to_broadcast((P, 2 * D))
                             ).then_inc(consts_in, 16)

                def load(k, p):
                    when(sp, mask_done, k - 1)
                    sp.dma_start(adjb[:, p, :], adj_t[:, k, :]).then_inc(adj_in[p], 16)

                for p in range(2):
                    sp.dma_start(xb[:, p, :], x_t[:, p, :]).then_inc(x_in[p], 16)
                    load(p, p)
                with sp.Fori(1, T // 2) as i:
                    for p in range(2):
                        load(i * 2 + p, p)

            @block.gpsimd
            def _(pool):
                def keep(k, p):
                    pool.wait_ge(compact, LINKS * (k + 1))
                    pool.tensor_copy(found[:, k, 0:S], first[:, p, :]).then_inc(first_kept, 1)
                    hold(pool, held["pool"], hp_copied, k + 1)
                    pool.dma_start(table_t[:, k, :], rowb[:, p, :]).then_inc(stored[p], 16)

                with pool.Fori(0, T // 2) as i:
                    for p in range(2):
                        keep(i * 2 + p, p)
                for p in range(2):
                    pool.wait_ge(stored[p], 16 * T // 2)

            @block.vector
            def _(dve):
                dve.memset(eps_c[:], EPS).then_inc(sets, 1)
                dve.memset(ones8[:], 1.0).then_inc(sets, 1)
                for p in range(2):
                    dve.memset(mask[:, p, :, SEG:SEG + TOP], 1.0).then_inc(sets, 1)
                dve.memset(share[:], 1.0 / N).then_inc(sets, 1)
                dve.memset(zero[:], 0.0).then_inc(sets, 1)
                dve.wait_ge(consts_in, 16 * NCONST)
                for c in range(ND):
                    for s in range(2):
                        n = 2 * c + s
                        if n:
                            dve.wait_ge(wa_done, n)
                        dve.tensor_tensor(wprod[:].rearrange("p (h f) -> p h f", h=H),
                                          wa[:, c, 0:D].rearrange("p (h f) -> p h f", h=H),
                                          a_bc[:, :, s, :], ALU.mult).then_inc(wprod_done, 1)
                        dve.wait_ge(wprod_done, n + 1)
                        dve.tensor_reduce(wa[:, c, D + s * H:D + (s + 1) * H],
                                          wprod[:].rearrange("p (h f) -> p h f", h=H),
                                          AX.X, ALU.add).then_inc(wa_done, 1)

                def statistics(k, p, half):
                    dve.wait_ge(x_in[p], 16 * half + 16)
                    dve.bn_stats(st[:, p, :], xb[:, p, :]).then_inc(stats, 1)
                    yield
                    hold(dve, held["dve"], stats, 3 * k + 1)
                    dve.bn_aggr(mv[:, p, :], st[:, p, :]).then_inc(stats, 1)
                    yield
                    dve.wait_ge(stats, 3 * k + 2)
                    dve.tensor_scalar(negm[:, p, :], mv[:, p, 0:1], -1.0, None, ALU.mult).then_inc(stats, 1)

                def shortlist(k, p):
                    dve.wait_ge(scanned, k + 1)
                    dve.tensor_tensor(rest[:, p, :], nth[:, p, :], base[:], ALU.add).then_inc(compact, 1)
                    yield
                    dve.wait_ge(compact, LINKS * k + 1)
                    dve.scalar_tensor_tensor(key[:, p, :], nth[:, p, :], float(SEG), rest[:, p, :],
                                             ALU.is_lt, ALU.mult).then_inc(compact, 1)
                    yield
                    hold_when(dve, held["dve"], first_kept, k - 1)
                    for r in range(S // TOP):
                        got = first[:, p, r * TOP:(r + 1) * TOP]
                        src, dst = (key, rest) if r % 2 == 0 else (rest, key)
                        hold(dve, held["dve"], compact, LINKS * k + 2 + 2 * r)
                        dve.max(got, src[:, p, :]).then_inc(compact, 1)
                        yield
                        if r + 1 < S // TOP:
                            hold(dve, held["dve"], compact, LINKS * k + 3 + 2 * r)
                            dve.match_replace(dst[:, p, :], got, src[:, p, :], 0.0).then_inc(compact, 1)
                            yield

                def scan(k, p, half, beside):
                    hold(dve, held["dve"], mask_done, k + 1)
                    for s in range(NS):
                        last = dve.max_index(nth[:, p, s * TOP:(s + 1) * TOP], ones8[:], mask[:, p, s, :])
                        if s == NS - 1:
                            last.then_inc(scanned, 1)
                        for steps in beside:
                            next(steps, None)
                    for steps in beside:
                        for _ in steps:
                            pass

                def tile(k, p, half, last=False):
                    beside = [] if last else [statistics(k + 1, 1 - p, half + p)]
                    if not isinstance(k, int) or k:
                        beside.append(shortlist(k - 1, 1 - p))
                    scan(k, p, half, beside)

                for _ in statistics(0, 0, 0):
                    pass
                for k in range(4):
                    tile(k, k % 2, k // 2)
                with dve.Fori(2, T // 2 - 1) as i:
                    for p in range(2):
                        tile(i * 2 + p, p, i)
                tile(T - 2, 0, T // 2 - 1)
                tile(T - 1, 1, T // 2 - 1, last=True)
                for _ in shortlist(T - 1, 1):
                    pass

            @block.scalar
            def _(act):
                load_exp_and_ln(nc, act)
                act.wait_ge(sets, 6)

                def masks(k, p, half):
                    act.wait_ge(adj_in[p], 16 * half + 16)
                    when(act, scanned, k - 1)
                    act.activation(mask[:, p, :, 0:SEG], adjb[:, p, :].rearrange("p (s n) -> p s n", s=NS),
                                   ACT.Relu, accum_out=found[:, k, S:S + 1]).then_inc(mask_done, 1)

                def normalise(k, p):
                    act.wait_ge(stats, 3 * k + 3)
                    act.activation(lnv[:, p, :], mv[:, p, 1:2], ACT.Ln, bias=eps_c[:]).then_inc(ln_chain, 1)
                    act.wait_ge(ln_chain, 3 * k + 1)
                    act.activation(rstd[:, p, :], lnv[:, p, :], ACT.Exp, scale=-0.5).then_inc(ln_chain, 1)
                    act.wait_ge(ln_chain, 3 * k + 2)
                    act.activation(nbias[:, p, :], negm[:, p, :], ACT.Copy, scale=rstd[:, p, :]
                                   ).then_inc(ln_chain, 1)
                    act.wait_ge(ln_chain, 3 * k + 3)
                    act.activation(hb[:, p, :], xb[:, p, :], ACT.Relu, bias=nbias[:, p, :],
                                   scale=rstd[:, p, :]).then_inc(h_done, 1)

                def load_x(k, p):
                    when(act, h_done, k - 1)
                    act.dma_start(xb[:, p, :], x_t[:, k, :]).then_inc(x_in[p], 16)

                def keep_hp(k, p):
                    act.wait_ge(proj_done, k + 1)
                    when(act, stored[p], (k - p) * 8)
                    act.activation(f_src[:, k, :], ps_f[p][:, 0:H], ACT.Copy)
                    act.activation(rowb[:, p, D:ROW], ps_f[p][:, H:2 * H], ACT.Copy)
                    act.activation(rowb[:, p, 0:D], ps_h[p][:], ACT.Copy).then_inc(hp_copied, 1)

                def keep_hT(k, p):
                    act.wait_ge(tr_done, k + 1)
                    act.activation(hT[:, p, :], ps_t[p][:], ACT.Copy).then_inc(hT_done, 1)

                def tile(k, p, more=True):
                    normalise(k, p)
                    if more:
                        load_x(k + 2, p)
                    if not isinstance(k, int) or k:
                        keep_hp(k - 1, 1 - p)
                    keep_hT(k, p)

                def pair(i, more=True):
                    for p in range(2):
                        masks(i * 2 + p, p, i)
                        tile(i * 2 + p, p, more)

                pair(0)
                pair(1)
                with act.Fori(2, T // 2 - 1) as i:
                    pair(i)
                pair(T // 2 - 1, more=False)
                keep_hp(T - 1, 1)
                act.wait_ge(meanT_ps, 1)
                act.activation(meanT[:], ps_m[:, 0:ND], ACT.Copy).then_inc(meanT_done, 1)
                act.wait_ge(mean_ps, 1)
                act.activation(mean_hp[:], ps_h[0][:], ACT.Copy)

            @block.tensor
            def _(pe):
                pe.wait_ge(consts_in, 16 * NCONST)
                pe.wait_ge(wa_done, 2 * ND)
                pe.wait_ge(sets, 6)
                pe.matmul(ps_m[:, 0:ND], zero[:], zero[:, 0:ND], start=True, stop=False)

                def tile(k, p, half):
                    pe.wait_ge(h_done, k + 1)
                    when(pe, hT_done, k - 1)
                    for c in range(ND):
                        last = pe.transpose(ps_t[p][:, c * P:(c + 1) * P], hb[:, p, c * P:(c + 1) * P], ident[:])
                    last.then_inc(tr_done, 1)
                    for c in range(ND):
                        pe.matmul(ps_m[:, c:c + 1], hb[:, p, c * P:(c + 1) * P], share[:],
                                  start=False, stop=False, skip_group_check=True)
                    pe.wait_ge(hT_done, k + 1)
                    when(pe, hp_copied, k - 1)
                    for c in range(ND):
                        pe.matmul(ps_h[p][:], hT[:, p, c * P:(c + 1) * P], wa[:, c, 0:D],
                                  start=c == 0, stop=c == ND - 1)
                    for c in range(ND):
                        last = pe.matmul(ps_f[p][:, 0:2 * H], hT[:, p, c * P:(c + 1) * P],
                                         wa[:, c, D:D + 2 * H], start=c == 0, stop=c == ND - 1)
                    last.then_inc(proj_done, 1)

                for p in range(2):
                    tile(p, p, 0)
                with pe.Fori(1, T // 2) as i:
                    for p in range(2):
                        tile(i * 2 + p, p, i)
                pe.matmul(ps_m[:, 0:ND], zero[:], zero[:, 0:ND], start=False, stop=True
                          ).then_inc(meanT_ps, 1)
                pe.wait_ge(meanT_done, 1)
                pe.wait_ge(hp_copied, T)
                for c in range(ND):
                    last = pe.matmul(ps_h[0][:], meanT[:, c:c + 1].to_broadcast((P, P)), wa[:, c, 0:D],
                                     start=c == 0, stop=c == ND - 1)
                last.then_inc(mean_ps, 1)

        nc.clear_and_free_semaphores(mine)
        nc.all_engine_barrier()


def sort_rows(nc, v_t, records, before_in, degrees_in, row_index, tile_key, bank, f_src, found, mean_v, flagged,
              n_flagged, g0, gkv):
    with ExitStack() as own:
        def sb(name, shape, dt=FP32):
            return own.enter_context(nc.sbuf_tensor(name, shape, dt))

        mine = []

        def sem(name):
            mine.append(nc.alloc_semaphore(name))
            return mine[-1]

        rec = sb("rec", [P, T, REC], I32)
        before = sb("before", [P, P], BF16)
        before_f = sb("before_f", [P, P])
        ones = sb("ones", [P, P], BF16)
        deg = sb("deg", [P, NDEG, T])
        keys = sb("keys", [P, T])
        row_of = sb("row_of", [P, T], I32)
        pad = sb("pad", [P, T, S])
        has = sb("has", [P, T, S])
        count = sb("count", [P, T])
        bad = sb("bad", [P, T], BF16)
        hot = sb("hot", [P, NDEG, T], BF16)
        total = sb("total", [P, NDEG * T])
        upto = sb("upto", [P, NDEG * T])
        nil = sb("nil", [P, NDEG * T])
        rank_f = sb("rank_f", [P, T])
        rank = sb("rank", [P, T], I32)
        fk = sb("fk", [P, 2, T])
        fl = sb("fl", [P, T])
        nf = sb("nf", [P, 1])
        share = sb("sort_share", [P, P])
        ps_c, ps_n, ps_f, ps_v = bank[0:2], bank[2:4], bank[4], bank[5]
        IN_VALUES = S + TWIN
        EARLY = T - IN_VALUES
        GROUPS = 4
        PER = IN_VALUES // GROUPS
        HALF = NDEG * T // 2

        in_ = sem("sort_in")
        early_in = sem("early_in")
        early_summed = sem("early_summed")
        values_in = [sem(f"values_in{g}") for g in range(GROUPS)]
        v_summed = sem("v_summed")
        chain = sem("sort_chain")
        sets = sem("sort_sets")
        hot_done = sem("hot_done")
        counted = sem("counted")
        rank_done = sem("rank_done")
        scattered = sem("scattered")

        with nc.Block() as block:
            @block.sync
            def _(sp):
                sp.dma_start(before_f[:], before_in).then_inc(in_, 16)
                sp.dma_start(deg[:].rearrange("p a t -> p (a t)"),
                             degrees_in.to_broadcast((P, NDEG * T))).then_inc(in_, 16)
                sp.dma_start(keys[:], tile_key.to_broadcast((P, T))).then_inc(in_, 16)
                sp.dma_start(row_of[:], row_index).then_inc(in_, 16)
                sp.dma_start(gkv[:, 0:EARLY, 0, :], v_t[:, 0:EARLY, 1, :]).then_inc(early_in, 16)
                for g in range(GROUPS):
                    sp.dma_start(gkv[:, g * PER:(g + 1) * PER, 1, :],
                                 v_t[:, EARLY + g * PER:EARLY + (g + 1) * PER, 1, :]).then_inc(values_in[g], 16)

            @block.vector
            def _(dve):
                links = [0]

                def link(ins):
                    links[0] += 1
                    ins.then_inc(chain, 1)
                    dve.wait_ge(chain, links[0])

                dve.tensor_copy(rec[:, :, R_FSRC:REC].bitcast(FP32), f_src[:])
                link(dve.tensor_scalar(has[:], found[:, :, 0:S], 0.0, None, ALU.is_gt))
                link(dve.reduce_sum(count[:], has[:], AX.X))
                dve.wait_ge(in_, 64)
                dve.tensor_copy(before[:], before_f[:])
                dve.tensor_copy(rec[:, :, R_ROW], row_of[:])
                dve.tensor_tensor(bad[:], count[:], found[:, :, S], ALU.not_equal)
                dve.tensor_tensor(hot[:], count[:, None, :].to_broadcast((P, NDEG, T)), deg[:], ALU.is_equal
                                  ).then_inc(hot_done, 1)
                dve.tensor_copy(rec[:, :, R_COUNT], count[:])
                link(dve.tensor_scalar(pad[:], found[:, :, 0:S], 0.0, float(NO_NODE + 1), ALU.is_equal, ALU.mult))
                link(dve.scalar_tensor_tensor(rec[:, :, 0:S], found[:, :, 0:S], -1.0, pad[:], ALU.add, ALU.add))
                dve.wait_ge(sets, 4)
                dve.wait_ge(counted, 1)
                for i in range(2):
                    last = dve.tensor_copy(total[:, i * HALF:(i + 1) * HALF], ps_n[i][:, 0:HALF])
                link(last)
                link(dve.tensor_tensor_scan(upto[:], total[:], nil[:], 0.0, ALU.add, ALU.add))
                link(dve.tensor_tensor(upto[:], upto[:], total[:], ALU.subtract))
                for i in range(2):
                    part = upto[:, i * HALF:(i + 1) * HALF]
                    last = dve.tensor_tensor(part, part, ps_c[i][:, 0:HALF], ALU.add)
                link(last)
                link(dve.tensor_tensor(upto[:], upto[:], hot[:].rearrange("p a t -> p (a t)"), ALU.mult))
                link(dve.reduce_sum(rank_f[:], upto[:].rearrange("p (a t) -> p t a", t=T), AX.X))
                dve.tensor_copy(rank[:], rank_f[:]).then_inc(rank_done, 1)
                link(dve.tensor_scalar(fl[:], ps_f[:, 0:T], 0.0, None, ALU.is_gt))
                link(dve.reduce_sum(nf[:], fl[:], AX.X))
                dve.tensor_copy(n_flagged[:], nf[0:1, :])
                link(dve.tensor_tensor(fk[:, 0, :], fl[:], keys[:], ALU.mult))
                for r in range(T // TOP):
                    link(dve.max(fl[:, r * TOP:(r + 1) * TOP], fk[:, r % 2, :]))
                    if r + 1 < T // TOP:
                        link(dve.match_replace(fk[:, (r + 1) % 2, :], fl[:, r * TOP:(r + 1) * TOP],
                                               fk[:, r % 2, :], 0.0))
                dve.tensor_scalar(flagged[:], fl[0:1, :], -1.0, 0.0, ALU.add, ALU.max)
                dve.wait_ge(early_summed, 1)
                dve.memset(gkv[:, :, 0, :], 0.0)

            @block.scalar
            def _(act):
                act.wait_ge(sets, 4)
                act.activation(g0[:], nil[:, None, 0:ROW].to_broadcast((P, S + TWIN, ROW)), ACT.Copy)
                act.wait_ge(v_summed, 1)
                act.activation(mean_v[:], ps_v[:], ACT.Copy)

            @block.tensor
            def _(pe):
                pe.wait_ge(sets, 4)
                pe.wait_ge(hot_done, 1)
                flat = hot[:].rearrange("p a t -> p (a t)")
                for i in range(2):
                    pe.matmul(ps_c[i][:, 0:HALF], before[:], flat[:, i * HALF:(i + 1) * HALF], start=True, stop=True)
                    pe.matmul(ps_n[i][:, 0:HALF], ones[:], flat[:, i * HALF:(i + 1) * HALF], start=True, stop=True)
                pe.matmul(ps_f[:, 0:T], ones[:], bad[:], start=True, stop=True).then_inc(counted, 1)
                pe.wait_ge(early_in, 16)
                for t in range(EARLY):
                    last = pe.matmul(ps_v[:], share[:], gkv[:, t, 0, :], start=t == 0, stop=False)
                last.then_inc(early_summed, 1)
                for g in range(GROUPS):
                    pe.wait_ge(values_in[g], 16)
                    for t in range(g * PER, (g + 1) * PER):
                        last = pe.matmul(ps_v[:], share[:], gkv[:, t, 1, :], start=False,
                                         stop=t == IN_VALUES - 1)
                last.then_inc(v_summed, 1)

            @block.gpsimd
            def _(pool):
                pool.memset(nil[:], 0.0).then_inc(sets, 1)
                pool.memset(ones[:], 1.0).then_inc(sets, 1)
                pool.memset(share[:], 1.0 / N).then_inc(sets, 1)
                pool.memset(rec[:, :, R_ROW + 1:R_FSRC], 0).then_inc(sets, 1)
                pool.wait_ge(sets, 4)
                pool.wait_ge(rank_done, 1)
                for t in range(T):
                    pool.indirect_dma_start(records, bass.IndirectOffsetOnAxis(rank[:, t:t + 1], 0),
                                            rec[:, t, :], None).then_inc(scattered, 16)
                pool.wait_ge(scattered, 16 * T)

        nc.clear_and_free_semaphores(mine)
        nc.all_engine_barrier()


def sparse_layers(nc, x, kv, table, records, out, psum, ident, eps_c, found, mean_hp, mean_v, held, g0, gkv):
    with ExitStack() as own:
        def sb(name, shape, dt=FP32):
            return own.enter_context(nc.sbuf_tensor(name, shape, dt))

        def sem(name):
            return own.enter_context(nc.semaphore(name))

        NCH = len(CHUNKS)
        srt = sb("srt", [P, T, REC], I32)
        srt_f = srt[:, :, R_FSRC:REC].bitcast(FP32)
        fill = found[:, :, 0:S]
        some = found[:, :, S:S + 1]
        none = sb("none", [P, T, 1])
        idx0 = sb("idx0", [P, 2, S + 2], I32)
        idx1 = sb("idx1", [P, 2, S], I32)
        idx_out = sb("idx_out", [P, 2, 1], I32)
        xs = sb("xs", [P, D])
        x1 = sb("x1", [P, 2, D])
        h1 = sb("h1", [P, 1, D])
        y = sb("y", [P, 2, D])
        em = sb("em", [P, D])
        sc = [sb(f"sc{layer}", [P, S, H]) for layer in range(2)]
        pr = [sb(f"pr{layer}", [P, S, H]) for layer in range(2)]
        al = [sb(f"al{layer}", [P, S, H]) for layer in range(2)]
        top = [sb(f"top{layer}", [P, H]) for layer in range(2)]
        den = [sb(f"den{layer}", [P, H]) for layer in range(2)]
        rden = [sb(f"rden{layer}", [P, H]) for layer in range(2)]
        bias = sb("bias", [P, S, H])
        diag = sb("diag", [P, 2, P])
        st = sb("st3", [P, 6])
        mv = sb("mv3", [P, 2])
        nrstd = sb("nrstd3", [P, 1])
        lnv = sb("lnv3", [P, 1])
        rstd = sb("rstd3", [P, 1])
        nbias = sb("nbias3", [P, 1])
        acc0, extra = psum[:, 0, :], psum[:, 1, :]
        acc1 = [psum[:, 2 + p, :] for p in range(2)]
        PART = 2
        qk = [psum[:, 4 + PART * r:4 + PART * (r + 1), :] for r in range(2)]
        qk_act = sb("qk_act", [P, PART, D])

        srt_in = sem("srt_in")
        cleared = sem("cleared")
        told = sem("told")
        idx_done = sem("idx_done")
        idx1_done = sem("idx1_done")
        idx_out_done = sem("idx_out_done")
        xs_in = sem("xs_in")
        g0_in = [[sem(f"g0_in{c}_{p}") for p in range(2 if s0 < TWIN else 1)] for c, (s0, _) in enumerate(CHUNKS)]
        g0_ready = sem("g0_ready")
        bias_done = sem("bias_done")
        g0_weighted = [sem(f"g0_weighted{c}") for c in range(NCH)]
        g0_free = [sem(f"g0_free{c}") for c in range(NCH)]
        kv_in = [[sem(f"kv_in{c}_{p}") for p in range(2 if s0 < TWIN else 1)] for c, (s0, _) in enumerate(CHUNKS)]
        aid_ready = sem("aid_ready")
        aid_summed = sem("aid_summed")
        aid_weighted = [sem(f"aid_weighted{layer}") for layer in range(2)]
        qk_done = [sem(f"qk_done{c}") for c in range(NCH)]
        v_weighted = [sem(f"v_weighted{c}") for c in range(NCH)]
        kv_free = [sem(f"kv_free{c}") for c in range(NCH)]
        soft = [sem(f"soft{layer}") for layer in range(2)]
        exp_done = [sem(f"exp_done{layer}") for layer in range(2)]
        LINKS = (8, 6)
        diag_done = sem("diag_done")
        acc0_done = sem("acc0_done")
        extra_done = sem("extra_done")
        acc1_done = sem("acc1_done")
        neg_done = sem("neg_done")
        em_done = sem("em_done")
        pos_done = sem("pos_done")
        fin = sem("fin")
        ln_chain = sem("ln_chain3")
        h1_done = sem("h1_done")
        y_done = sem("y_done")
        out_stored = [sem(f"out_stored{p}") for p in range(2)]

        def slots(engine, k):
            return engine.value_load(srt[0:1, k, R_COUNT:R_COUNT + 1], min_val=0, max_val=S)

        def over_chunks(engine, n, work, start=0, stop=S):
            with ExitStack() as nest:
                for c, (s0, m) in enumerate(CHUNKS):
                    if start <= s0 < stop:
                        if c:
                            nest.enter_context(engine.If(n > s0))
                        work(c, s0, m)

        def place(s, p):
            return s + p * TWIN if s < TWIN else s + TWIN

        def of(t, k):
            return t[:, k:k + 1] if isinstance(k, int) else t[:, bass.ds(k, 1)]

        def tiles(engine, step):
            for k in range(2):
                step(k, k, 0)
            with engine.Fori(1, T // 2 - 1) as i:
                for p in range(2):
                    step(i * 2 + p, p, i)
            step(T - 2, 0, T // 2 - 1, last=True)

        with nc.Block() as block:
            @block.sync
            def _(sp):
                sp.dma_start(srt[:], records.rearrange("(t p) r -> p t r", p=P)).then_inc(srt_in, 16)

            @block.gpsimd
            def _(pool):
                pool.wait_ge(srt_in, 16)
                pool.wait_ge(told, 3)

                def fetch0(k, p):
                    hold_when(pool, held["pool"], h1_done, k - 1)
                    pool.tensor_copy(idx0[:, p, :], srt[:, k, 0:S + 2]).then_inc(idx_done, 1)
                    n = slots(pool, k)
                    hold(pool, held["pool"], idx_done, k + 1)
                    def gather(c, s0, m):
                        hold_when(pool, held["pool"], g0_free[c], k - 1 if s0 < TWIN else k)
                        for s in range(s0, s0 + m):
                            pool.indirect_dma_start(g0[:, place(s, p), :], None, table,
                                                    bass.IndirectOffsetOnAxis(idx0[:, p, s:s + 1], 0),
                                                    bounds_check=N - 1, oob_is_err=False
                                                    ).then_inc(g0_in[c][p if s0 < TWIN else 0], 16)
                    over_chunks(pool, n, gather)
                    hold_when(pool, held["pool"], exp_done[0], k)
                    pool.tensor_tensor(bias[:], of(fill, k).rearrange("p o s -> p s o").to_broadcast((P, S, H)),
                                       of(srt_f, k).to_broadcast((P, S, H)), ALU.add).then_inc(bias_done, 1)

                def fetch_x(k, p):
                    hold_when(pool, held["pool"], h1_done, k)
                    pool.indirect_dma_start(xs[:], None, x,
                                            bass.IndirectOffsetOnAxis(idx0[:, p, R_ROW:R_ROW + 1], 0)
                                            ).then_inc(xs_in, 16)

                def await0(k, p, half):
                    def arrived(c, s0, m):
                        if s0 < TWIN:
                            hold(pool, held["pool"], g0_in[c][p], (half + 1) * (16 * m))
                        else:
                            hold(pool, held["pool"], g0_in[c][0], (k + 1) * (16 * m))
                    over_chunks(pool, slots(pool, k), arrived)
                    pool.sem_inc(g0_ready, 1)

                def fetch1(k, p, n, **part):
                    def gather(c, s0, m):
                        hold_when(pool, held["pool"], kv_free[c], k - 1 if s0 < TWIN else k)
                        for s in range(s0, s0 + m):
                            pool.indirect_dma_start(
                                gkv[:, place(s, p), :, :].rearrange("p k d -> p (k d)"), None, kv,
                                bass.IndirectOffsetOnAxis(idx1[:, p, s:s + 1], 0),
                                bounds_check=N - 1, oob_is_err=False
                                ).then_inc(kv_in[c][p if s0 < TWIN else 0], 16)
                    over_chunks(pool, n, gather, **part)

                def first1(k, p):
                    hold_when(pool, held["pool"], exp_done[1], k - 1)
                    pool.tensor_copy(idx1[:, p, :], srt[:, k, 0:S]).then_inc(idx1_done, 1)
                    hold(pool, held["pool"], idx1_done, k + 1)
                    fetch1(k, p, slots(pool, k), stop=TWIN)

                def rest1(k, p):
                    fetch1(k, p, slots(pool, k), start=TWIN)

                def store(k, p):
                    hold(pool, held["pool"], y_done, k + 1)
                    pool.tensor_copy(idx_out[:, p, :], srt[:, k, R_ROW:R_ROW + 1]).then_inc(idx_out_done, 1)
                    hold(pool, held["pool"], idx_out_done, k + 1)
                    pool.indirect_dma_start(out, bass.IndirectOffsetOnAxis(idx_out[:, p, :], 0),
                                            y[:, p, :], None).then_inc(out_stored[p], 16)

                def step(k, p, half, last=False):
                    first1(k + 1, 1 - p)
                    if not last:
                        fetch0(k + 2, p)
                    if not isinstance(k, int) or k:
                        store(k - 1, 1 - p)
                    if not last:
                        await0(k + 2, p, half + 1)
                    rest1(k + 1, 1 - p)
                    if not last:
                        fetch_x(k + 2, p)

                fetch0(0, 0)
                fetch_x(0, 0)
                await0(0, 0, 0)
                first1(0, 0)
                rest1(0, 0)
                fetch0(1, 1)
                await0(1, 1, 0)
                fetch_x(1, 1)
                tiles(pool, step)
                store(T - 2, 0)
                store(T - 1, 1)
                for p in range(2):
                    pool.wait_ge(out_stored[p], 16 * T // 2)

            @block.vector
            def _(dve):
                for layer in range(2):
                    dve.memset(sc[layer][:], 0.0).then_inc(cleared, 1)
                dve.wait_ge(cleared, 2)
                hold(dve, held["dve"], srt_in, 16)
                dve.tensor_scalar(fill, srt[:, :, 0:S], float(N), NEG_FILL, ALU.is_ge, ALU.mult).then_inc(told, 1)
                dve.tensor_scalar(some, srt[:, :, R_COUNT:R_COUNT + 1], 0.0, None, ALU.is_gt).then_inc(told, 1)
                dve.tensor_scalar(none[:], srt[:, :, R_COUNT:R_COUNT + 1], 0.0, None, ALU.is_equal
                                  ).then_inc(told, 1)
                dve.wait_ge(told, 3)

                def by_head(t):
                    return t[:].rearrange("p s h -> p h s")

                def over_slots(t):
                    return t[:, None, :].to_broadcast((P, S, H))

                def query_keys(k, p, half, n):
                    dve.wait_ge(h1_done, k + 1)
                    def work(c, s0, m):
                        if s0 < TWIN:
                            dve.wait_ge(kv_in[c][p], (half + 1) * (16 * m))
                        else:
                            dve.wait_ge(kv_in[c][0], (k + 1) * (16 * m))
                        aided = PART if c == 0 else 0
                        if aided:
                            dve.tensor_tensor(qk_act[:], gkv[:, place(s0, p):place(s0, p) + PART, 0, :],
                                              h1[:].to_broadcast((P, PART, D)), ALU.mult).then_inc(aid_ready, 1)
                        parts = (m - aided) // PART
                        first = s0 + aided
                        for r in range(parts):
                            at = place(first + r * PART, p)
                            dve.tensor_tensor(qk[(first // PART + r) % 2], gkv[:, at:at + PART, 0, :],
                                              h1[:].to_broadcast((P, PART, D)), ALU.mult).then_inc(qk_done[c], 1)
                        for r in range(parts):
                            dve.wait_ge(qk_done[c], k * (2 * parts) + r + 1)
                            dve.tensor_reduce(sc[1][:, first + r * PART:first + (r + 1) * PART, :],
                                              qk[(first // PART + r) % 2].rearrange("p s (h f) -> p s h f", h=H),
                                              AX.X, ALU.add).then_inc(qk_done[c], 1)
                        hold(dve, held["dve"], qk_done[c], (k + 1) * (2 * parts))
                    over_chunks(dve, n, work)
                    dve.wait_ge(aid_summed, k + 1)
                    dve.tensor_tensor(sc[1][:], sc[1][:],
                                      of(fill, k).rearrange("p o s -> p s o").to_broadcast((P, S, H)), ALU.add
                                      ).then_inc(soft[1], 1)
                    dve.wait_ge(soft[1], k * LINKS[1] + 1)

                def prepare(k, p):
                    dve.wait_ge(bias_done, k + 1)
                    dve.wait_ge(g0_ready, k + 1)
                    for a, b in ((0, TWIN), (TWIN, S)):
                        dve.tensor_tensor(sc[0][:, a:b, :], g0[:, place(a, p):place(b - 1, p) + 1, D:ROW],
                                          bias[:, a:b, :], ALU.add).then_inc(soft[0], 1)
                    dve.wait_ge(soft[0], k * LINKS[0] + 2)
                    dve.scalar_tensor_tensor(sc[0][:], sc[0][:], ALPHA, sc[0][:], ALU.mult, ALU.max
                                             ).then_inc(soft[0], 1)
                    dve.wait_ge(soft[0], k * LINKS[0] + 3)

                def shift(layer, k, at):
                    dve.reduce_max(top[layer][:], by_head(sc[layer]), AX.X).then_inc(soft[layer], 1)
                    dve.wait_ge(soft[layer], k * LINKS[layer] + at + 1)
                    dve.tensor_tensor(sc[layer][:], sc[layer][:], over_slots(top[layer]), ALU.subtract
                                      ).then_inc(soft[layer], 1)

                def attention(layer, k, at):
                    dve.wait_ge(exp_done[layer], k + 1)
                    dve.reduce_sum(den[layer][:], by_head(pr[layer]), AX.X).then_inc(soft[layer], 1)
                    dve.wait_ge(soft[layer], k * LINKS[layer] + at + 1)
                    dve.reciprocal(rden[layer][:], den[layer][:]).then_inc(soft[layer], 1)
                    dve.wait_ge(soft[layer], k * LINKS[layer] + at + 2)
                    dve.scalar_tensor_tensor(al[layer][:], pr[layer][:], some[:, k, :], over_slots(rden[layer]),
                                             ALU.mult, ALU.mult).then_inc(soft[layer], 1)
                    dve.wait_ge(soft[layer], k * LINKS[layer] + at + 3)

                def weigh(layer, k, p, n):
                    def work(c, s0, m):
                        a, b = s0 + (AIDED[layer] if c == 0 else 0), s0 + m
                        at = place(a, p)
                        rows = g0[:, at:at + b - a, 0:D] if layer == 0 else gkv[:, at:at + b - a, 1, :]
                        rows = rows.rearrange("p s (h f) -> p s h f", h=H)
                        dve.tensor_tensor(rows, rows, al[layer][:, a:b, :, None].to_broadcast((P, b - a, H, F)),
                                          ALU.mult).then_inc((g0_weighted, v_weighted)[layer][c], 1)
                    over_chunks(dve, n, work)

                def finish0(k, p):
                    dve.wait_ge(extra_done, k + 1)
                    dve.wait_ge(pos_done, k + 1)
                    dve.tensor_tensor(x1[:, p, :], x1[:, p, :], extra, ALU.add).then_inc(fin, 1)

                def statistics(k, p):
                    dve.wait_ge(fin, k * 3 + 1)
                    dve.bn_stats(st[:], x1[:, p, :]).then_inc(fin, 1)
                    hold(dve, held["dve"], fin, k * 3 + 2)
                    dve.bn_aggr(mv[:], st[:]).then_inc(fin, 1)

                def layer0(k, p):
                    prepare(k, p)
                    shift(0, k, 3)
                    n = slots(dve, k)
                    attention(0, k, 5)
                    weigh(0, k, p, n)

                def layer1(k, p, half, beside=None):
                    n = slots(dve, k)
                    query_keys(k, p, half, n)
                    shift(1, k, 1)
                    if beside:
                        beside()
                    attention(1, k, 3)
                    weigh(1, k, p, n)

                def step(k, p, half, last=False):
                    if isinstance(k, int) and k == 0:
                        layer1(0, 0, 0, lambda: layer0(1, 1))
                        finish0(1, 1)
                    else:
                        layer1(k, p, half, lambda: finish0(k + 1, 1 - p))
                    statistics(k + 1, 1 - p)
                    if not last:
                        layer0(k + 2, p)

                layer0(0, 0)
                finish0(0, 0)
                statistics(0, 0)
                tiles(dve, step)
                layer1(T - 1, 1, T // 2 - 1)

            @block.scalar
            def _(act):
                act.wait_ge(told, 3)

                def exponentials(layer, k):
                    act.wait_ge(soft[layer], k * LINKS[layer] + (5, 3)[layer])
                    act.activation(pr[layer][:], sc[layer][:], ACT.Exp, scale=(1.0, SCALE)[layer]
                                   ).then_inc(exp_done[layer], 1)

                def add_up_products(k):
                    act.wait_ge(aid_ready, k + 1)
                    for s in range(PART):
                        for h in range(H):
                            part = qk_act[:, s, h * F:(h + 1) * F]
                            last = act.activation(part, part, ACT.Copy, accum_out=sc[1][:, s, h:h + 1])
                    last.then_inc(aid_summed, 1)

                def weigh(layer, k, p):
                    act.wait_ge(soft[layer], k * LINKS[layer] + LINKS[layer])
                    for s in range(AIDED[layer]):
                        for h in range(H):
                            at = place(s, p)
                            row = g0[:, at, :] if layer == 0 else gkv[:, at, 1, :]
                            row = row[:, h * F:(h + 1) * F]
                            last = act.activation(row, row, ACT.Copy, scale=al[layer][:, s, h:h + 1])
                    last.then_inc(aid_weighted[layer], 1)

                def negative_part(k, p):
                    act.wait_ge(acc0_done, k + 1)
                    act.activation(em[:], acc0, ACT.Relu, scale=-1.0).then_inc(neg_done, 1)
                    act.wait_ge(neg_done, k + 1)
                    act.activation(em[:], em[:], ACT.Exp, scale=-1.0).then_inc(em_done, 1)
                    when(act, acc1_done, k - 1)
                    act.activation(x1[:, p, :], acc0, ACT.Relu).then_inc(pos_done, 1)

                def normalise(k, p):
                    act.wait_ge(fin, k * 3 + 3)
                    act.activation(lnv[:], mv[:, 1:2], ACT.Ln, bias=eps_c[:]).then_inc(ln_chain, 1)
                    act.wait_ge(ln_chain, k * 4 + 1)
                    act.activation(rstd[:], lnv[:], ACT.Exp, scale=-0.5).then_inc(ln_chain, 1)
                    act.wait_ge(ln_chain, k * 4 + 2)
                    act.activation(nrstd[:], rstd[:], ACT.Copy, scale=-1.0).then_inc(ln_chain, 1)
                    act.wait_ge(ln_chain, k * 4 + 3)
                    act.activation(nbias[:], mv[:, 0:1], ACT.Copy, scale=nrstd[:]).then_inc(ln_chain, 1)
                    act.wait_ge(ln_chain, k * 4 + 4)
                    act.activation(h1[:, 0, :], x1[:, p, :], ACT.Relu, bias=nbias[:], scale=rstd[:]
                                   ).then_inc(h1_done, 1)

                def diagonal(k, p):
                    act.activation(diag[:, p, :], ident[:], ACT.Copy, scale=none[:, k, :]).then_inc(diag_done, 1)

                def output(k, p, half):
                    act.wait_ge(acc1_done, k + 1)
                    when(act, out_stored[p], 16 * half)
                    act.activation(y[:, p, :], acc1[p], ACT.Copy, bias=-1.0).then_inc(y_done, 1)

                def step(k, p, half, last=False):
                    add_up_products(k)
                    if isinstance(k, int) and k == 0:
                        exponentials(1, 0)
                        exponentials(0, 1)
                        weigh(0, 1, 1)
                        diagonal(1, 1)
                        weigh(1, 0, 0)
                        negative_part(1, 1)
                    else:
                        negative_part(k + 1, 1 - p)
                        exponentials(1, k)
                        weigh(1, k, p)
                    normalise(k + 1, 1 - p)
                    if not last:
                        exponentials(0, k + 2)
                        weigh(0, k + 2, p)
                    output(k, p, half)
                    if not last:
                        diagonal(k + 2, p)

                exponentials(0, 0)
                weigh(0, 0, 0)
                diagonal(0, 0)
                negative_part(0, 0)
                normalise(0, 0)
                tiles(act, step)
                add_up_products(T - 1)
                exponentials(1, T - 1)
                weigh(1, T - 1, 1)
                output(T - 1, 1, T // 2 - 1)

            @block.tensor
            def _(pe):
                pe.wait_ge(srt_in, 16)

                def add_up(layer, k, n, acc, weighted, free, rows):
                    def add(c, s0, m):
                        pe.wait_ge(weighted[c], k + 1)
                        first = AIDED[layer] if c == 0 else s0
                        for s in range(first, s0 + m):
                            last = pe.matmul(acc, ident[:], rows(s), start=s == AIDED[layer], stop=False)
                        if c:
                            last.then_inc(free[c], 1)
                    over_chunks(pe, n, add)
                    pe.wait_ge(aid_weighted[layer], k + 1)
                    for s in range(AIDED[layer]):
                        last = pe.matmul(acc, ident[:], rows(s), start=False, stop=False)
                    last.then_inc(free[0], 1)

                def layer0(k, p, n):
                    when(pe, fin, k * 3 - 2)
                    add_up(0, k, n, acc0, g0_weighted, g0_free, lambda s: g0[:, place(s, p), 0:D])
                    pe.wait_ge(diag_done, k + 1)
                    pe.matmul(acc0, diag[:, p, :], mean_hp[:], start=False, stop=True
                              ).then_inc(acc0_done, 1)

                def add_x(k):
                    pe.wait_ge(xs_in, k * 16 + 16)
                    pe.matmul(extra, ident[:], xs[:], start=True, stop=False)
                    pe.wait_ge(em_done, k + 1)
                    pe.matmul(extra, ident[:], em[:], start=False, stop=True).then_inc(extra_done, 1)

                def layer1(k, p, n):
                    when(pe, y_done, k - 1)
                    add_up(1, k, n, acc1[p], v_weighted, kv_free, lambda s: gkv[:, place(s, p), 1, :])
                    pe.matmul(acc1[p], diag[:, p, :], mean_v[:], start=False, stop=False)
                    pe.matmul(acc1[p], ident[:], x1[:, p, :], start=False, stop=True).then_inc(acc1_done, 1)

                def step(k, p, half, last=False):
                    add_x(k + 1)
                    layer1(k, p, slots(pe, k))
                    if not last:
                        layer0(k + 2, p, slots(pe, k + 2))

                layer0(0, 0, slots(pe, 0))
                add_x(0)
                layer0(1, 1, slots(pe, 1))
                tiles(pe, step)
                layer1(T - 1, 1, slots(pe, T - 1))


def dense_layers(nc, x_t, adj_t, table_t, kv_t, out_t, bank, ident, eps_c, f_src, held, flagged, n_flagged):
    ctx = ExitStack()
    with ctx:
        def sb(name, shape, dt=FP32):
            return ctx.enter_context(nc.sbuf_tensor(name, shape, dt))

        def sem(name):
            return ctx.enter_context(nc.semaphore(name))

        hp = sb("g_hp", [P, T, ROW])
        kvh = sb("g_kvh", [P, T, 2, F])
        val = sb("g_val", [P, T, F])
        fdc = sb("g_fdc", [P, T])
        fill = sb("g_fill", [P, N])
        adj_b = fill[:].bitcast(I32)
        e = sb("g_e", [P, N])
        pT = sb("g_pT", [P, N])
        kT = pT
        x0 = sb("g_x0", [P, D])
        o = sb("g_o", [P, D])
        t0 = sb("g_t0", [P, D])
        t0n = sb("g_t0n", [P, D])
        t0e = sb("g_t0e", [P, D])
        h1 = sb("g_h1", [P, D])
        q = sb("g_q", [P, F])
        qT = sb("g_qT", [F, P])
        st = sb("g_st", [P, 6])
        mv = sb("g_mv", [P, 2])
        lnv = sb("g_lnv", [P, 1])
        rstd = sb("g_rstd", [P, 1])
        nb = sb("g_nb", [P, 1])
        nm = sb("g_nm", [P, 1])
        den = sb("g_den", [P, 1])
        rden = sb("g_rden", [P, 1])
        ps_e, ps_t, ps_o = bank[0:2], bank[2:4], bank[4]
        ps_q = bank[5]

        table_in = sem("g_table_in")
        xa_in = sem("g_xa_in")
        fill_done = sem("g_fill_done")
        tile_done = sem("g_tile_done")
        out_stored = sem("g_out_stored")
        elu_neg = sem("g_elu_neg")
        elu_exp = sem("g_elu_exp")
        acc0 = sem("g_acc0")
        x1_done = sem("g_x1_done")
        stats = sem("g_stats")
        lnd = sem("g_lnd")
        rstd_done = sem("g_rstd_done")
        nb_done = sem("g_nb_done")
        h1_done = sem("g_h1_done")

        names = ("head", "kv_in", "kT_ps", "kT", "qT_ps", "qT", "block", "read", "leaky", "masked",
                 "top", "shift", "exp", "pT_ps", "pT", "weighted", "rden", "out")
        s0, s1 = [{n: sem(f"g{layer}_{n}") for n in names} for layer in range(2)]

        with nc.Block() as block:
            @block.sync
            def _(sp):
                sp.sem_inc(out_stored, 1)
                n = sp.value_load(n_flagged[:], min_val=0, max_val=T)
                with sp.If(n > 0):
                    sp.dma_start(hp[:], table_t).then_inc(table_in, 16)
                    with sp.Fori(0, n) as g:
                        t = sp.value_load(flagged[0:1, bass.ds(g, 1)], min_val=0, max_val=T - 1)
                        sp.wait_ge(tile_done, g + 1)
                        sp.dma_start(x0[:], x_t[:, t, :]).then_inc(xa_in, 16)
                        sp.dma_start(adj_b, adj_t[:, t, :]).then_inc(xa_in, 16)
                        with sp.Fori(0, H) as h:
                            sp.wait_ge(s1["weighted"], g * H + h + 1)
                            for k in range(2):
                                sp.dma_start(kvh[:, :, k, :], kv_t[:, :, k, h, :]).then_inc(s1["kv_in"], 16)
                        sp.wait_ge(tile_done, g + 2)
                        sp.dma_start(out_t[:, t, :], t0[:]).then_inc(out_stored, 16)
                    hold(sp, held["sp"], out_stored, n * 16 + 1)

            @block.vector
            def _(dve):
                dve.sem_inc(tile_done, 1)
                dve.sem_inc(s0["out"], 1)
                dve.sem_inc(s1["out"], 1)
                def attend(s, u, h):
                    dve.scalar_tensor_tensor(e[:], fill[:], NEG_FILL, e[:], ALU.add, ALU.min
                                             ).then_inc(s["masked"], 1)
                    dve.wait_ge(s["masked"], u + 1)
                    dve.reduce_max(nm[:], e[:], AX.X).then_inc(s["top"], 1)
                    dve.wait_ge(s["top"], u + 1)
                    dve.tensor_scalar(nm[:], nm[:], -1.0 if s is s0 else -SCALE, None, ALU.mult
                                      ).then_inc(s["shift"], 1)
                    dve.wait_ge(s["exp"], u + 1)
                    dve.reciprocal(rden[:], den[:]).then_inc(s["rden"], 1)
                    dve.wait_ge(s["rden"], u + 1)
                    dve.wait_ge(s["weighted"], u + 2)
                    dve.tensor_scalar(o[:, bass.ds(h * F, F)], ps_o[:, 0:F], rden[:], None, ALU.mult
                                      ).then_inc(s["out"], 1)

                n = dve.value_load(n_flagged[:], min_val=0, max_val=T)
                with dve.If(n > 0):
                    dve.wait_ge(table_in, 16)
                    with dve.Fori(0, n) as g:
                        t = dve.value_load(flagged[0:1, bass.ds(g, 1)], min_val=0, max_val=T - 1)
                        dve.wait_ge(xa_in, g * 32 + 32)
                        dve.tensor_scalar(fill[:], adj_b, 0.0, BIG, ALU.is_gt, ALU.mult).then_inc(fill_done, 1)
                        with dve.Fori(0, H) as h:
                            u = g * H + h
                            dve.wait_ge(s0["weighted"], u + 1)
                            dve.tensor_copy(val[:], hp[:, :, bass.ds(h * F, F)]).then_inc(s0["head"], 1)
                            dve.tensor_copy(fdc[:], hp[:, :, bass.ds(h + D, 1)].rearrange("p t o -> p (t o)")
                                            ).then_inc(s0["head"], 1)
                            for b in range(NB):
                                dve.wait_ge(s0["block"], u * NB + b + 1)
                                dve.tensor_scalar(e[:, b * BLK:(b + 1) * BLK], ps_e[b % 2][:],
                                                  f_src[:, t, bass.ds(h, 1)], None, ALU.add
                                                  ).then_inc(s0["read"], 1)
                            dve.wait_ge(s0["read"], u * NB + NB + 2)
                            dve.scalar_tensor_tensor(e[:], e[:], ALPHA, e[:], ALU.mult, ALU.max
                                                     ).then_inc(s0["leaky"], 1)
                            dve.wait_ge(s0["leaky"], u + 1)
                            dve.wait_ge(fill_done, g + 1)
                            attend(s0, u, h)
                        dve.wait_ge(elu_exp, g + 1)
                        dve.wait_ge(out_stored, g * 16 + 1)
                        dve.scalar_tensor_tensor(t0[:], o[:], 0.0, t0e[:], ALU.max, ALU.add).then_inc(acc0, 1)
                        dve.wait_ge(acc0, g + 1)
                        dve.scalar_tensor_tensor(x0[:], t0[:], -1.0, x0[:], ALU.add, ALU.add).then_inc(x1_done, 1)
                        dve.wait_ge(x1_done, g + 1)
                        dve.bn_stats(st[:], x0[:]).then_inc(stats, 1)
                        hold(dve, held["dve"], stats, 2 * g + 1)
                        dve.bn_aggr(mv[:], st[:]).then_inc(stats, 1)
                        dve.wait_ge(stats, 2 * g + 2)
                        dve.wait_ge(rstd_done, g + 1)
                        dve.tensor_scalar(nb[:], mv[:, 0:1], rstd[:], -1.0, ALU.mult, ALU.mult).then_inc(nb_done, 1)
                        hold(dve, held["dve"], h1_done, g + 1)
                        with dve.Fori(0, H) as h:
                            u = g * H + h
                            dve.wait_ge(s1["weighted"], u + 1)
                            dve.tensor_copy(q[:], h1[:, bass.ds(h * F, F)]).then_inc(s1["head"], 1)
                            for b in range(NB):
                                dve.wait_ge(s1["block"], u * NB + b + 1)
                                dve.tensor_copy(e[:, b * BLK:(b + 1) * BLK], ps_e[b % 2][:]).then_inc(s1["read"], 1)
                            dve.wait_ge(s1["read"], u * NB + NB + 2)
                            attend(s1, u, h)
                        dve.wait_ge(s1["out"], (g + 1) * H + 1)
                        dve.tensor_tensor(t0[:], o[:], x0[:], ALU.add).then_inc(tile_done, 1)

            @block.scalar
            def _(act):
                def attend(s, u):
                    act.wait_ge(s["shift"], u + 1)
                    act.activation(e[:], e[:], ACT.Exp, bias=nm[:], scale=1.0 if s is s0 else SCALE,
                                   accum_out=den[:]).then_inc(s["exp"], 1)
                    for b in range(NB):
                        act.wait_ge(s["pT_ps"], u * NB + b + 1)
                        act.activation(pT[:, b * BLK:(b + 1) * BLK], ps_t[b % 2][:], ACT.Copy
                                       ).then_inc(s["pT"], 1)

                for s in (s0, s1):
                    act.sem_inc(s["pT"], 2)
                act.sem_inc(s1["kT"], 2)
                n = act.value_load(n_flagged[:], min_val=0, max_val=T)
                with act.If(n > 0):
                    with act.Fori(0, n) as g:
                        with act.Fori(0, H) as h:
                            attend(s0, g * H + h)
                        act.wait_ge(s0["out"], (g + 1) * H + 1)
                        act.activation(t0n[:], o[:], ACT.Relu, scale=-1.0).then_inc(elu_neg, 1)
                        act.wait_ge(elu_neg, g + 1)
                        act.activation(t0e[:], t0n[:], ACT.Exp, scale=-1.0).then_inc(elu_exp, 1)
                        act.wait_ge(stats, 2 * g + 2)
                        act.activation(lnv[:], mv[:, 1:2], ACT.Ln, bias=eps_c[:]).then_inc(lnd, 1)
                        act.wait_ge(lnd, g + 1)
                        act.activation(rstd[:], lnv[:], ACT.Exp, scale=-0.5).then_inc(rstd_done, 1)
                        act.wait_ge(nb_done, g + 1)
                        act.activation(h1[:], x0[:], ACT.Relu, bias=nb[:], scale=rstd[:]).then_inc(h1_done, 1)
                        with act.Fori(0, H) as h:
                            u = g * H + h
                            act.wait_ge(s1["qT_ps"], u + 1)
                            act.activation(qT[:], ps_q[0:F, 0:P], ACT.Copy).then_inc(s1["qT"], 1)
                            for b in range(NB):
                                act.wait_ge(s1["kT_ps"], u * NB + b + 1)
                                act.activation(kT[0:F, b * BLK:(b + 1) * BLK], ps_t[b % 2][0:F, :], ACT.Copy
                                               ).then_inc(s1["kT"], 1)
                            attend(s1, u)

            @block.tensor
            def _(pe):
                PB = BLK // P
                for s in (s0, s1):
                    pe.sem_inc(s["weighted"], 1)

                def attend(s, u, values):
                    pe.wait_ge(s["exp"], u + 1)
                    for b in range(NB):
                        pe.wait_ge(s["pT"], u * NB + b + 1)
                        for c in range(PB):
                            j = b * PB + c
                            last = pe.transpose(ps_t[b % 2][:, c * P:(c + 1) * P], e[:, j * P:(j + 1) * P], ident[:])
                        last.then_inc(s["pT_ps"], 1)
                    pe.wait_ge(s["pT"], u * NB + NB + 2)
                    pe.wait_ge(s["out"], u + 1)
                    for j in range(T):
                        last = pe.matmul(ps_o[:, 0:F], pT[:, j * P:(j + 1) * P], values(j),
                                         start=j == 0, stop=j == T - 1)
                    last.then_inc(s["weighted"], 1)

                n = pe.value_load(n_flagged[:], min_val=0, max_val=T)
                with pe.If(n > 0):
                    pe.wait_ge(table_in, 16)
                    with pe.Fori(0, n) as g:
                        with pe.Fori(0, H) as h:
                            u = g * H + h
                            pe.wait_ge(s0["head"], 2 * u + 2)
                            for b in range(NB):
                                pe.wait_ge(s0["read"], u * NB + b + 1)
                                for c in range(PB):
                                    j = b * PB + c
                                    last = pe.matmul(ps_e[b % 2][:, c * P:(c + 1) * P],
                                                     fdc[:, j:j + 1].to_broadcast((P, P)), ident[:],
                                                     start=True, stop=True)
                                last.then_inc(s0["block"], 1)
                            attend(s0, u, lambda j: val[:, j, :])
                        with pe.Fori(0, H) as h:
                            u = g * H + h
                            hold(pe, held["pe"], s1["head"], u + 1)
                            pe.transpose(ps_q[0:F, 0:P], q[:], ident[:]).then_inc(s1["qT_ps"], 1)
                            pe.wait_ge(s1["kv_in"], 32 * u + 32)
                            for b in range(NB):
                                hold(pe, held["pe"], s1["kT"], u * NB + b + 1)
                                for c in range(PB):
                                    j = b * PB + c
                                    last = pe.transpose(ps_t[b % 2][0:F, c * P:(c + 1) * P], kvh[:, j, 0, :], ident[:])
                                last.then_inc(s1["kT_ps"], 1)
                            pe.wait_ge(s1["qT"], u + 1)
                            for b in range(NB):
                                pe.wait_ge(s1["kT"], u * NB + b + 3)
                                pe.wait_ge(s1["read"], u * NB + b + 1)
                                pe.matmul(ps_e[b % 2][:], qT[:], kT[0:F, b * BLK:(b + 1) * BLK],
                                          start=True, stop=True).then_inc(s1["block"], 1)
                            attend(s1, u, lambda j: kvh[:, j, 1, :])

            @block.gpsimd
            def _(pool):
                pool.sem_inc(s0["read"], 2)
                pool.sem_inc(s1["read"], 2)


def kernel(x, adj, L0_gnn_W, L0_gnn_a, L1_gnn_x2, L1_gnn_v):
    import numpy as np
    import concourse.bacc as bacc
    from concourse.bass_utils import run_bass_kernel_spmd

    arrays = {
        "x": np.ascontiguousarray(x),
        "adj": np.ascontiguousarray(adj),
        "kv": np.concatenate([L1_gnn_x2, L1_gnn_v], axis=1),
        "w": np.ascontiguousarray(np.transpose(L0_gnn_W, (1, 0, 2)).reshape(D, D)),
        "a": np.ascontiguousarray(L0_gnn_a),
        "eye": np.eye(P, dtype=np.float32),
        "before": np.triu(np.ones((P, P), np.float32), 1),
        "seg_base": np.tile(np.repeat(np.arange(NS, dtype=np.float32) * SEG + 1, TOP), (P, 1)),
        "degrees": np.repeat(np.arange(S, -1, -1, dtype=np.float32), T)[None],
        "row_index": np.arange(N, dtype=np.int32).reshape(T, P).T.copy(),
        "tile_key": np.arange(1, T + 1, dtype=np.float32)[None],
    }
    nc = bacc.Bacc("TRN2", target_bir_lowering=False, num_devices=1)
    args = {n: nc.dram_tensor(f"in_{n}", v.shape, mybir.dt.from_np(v.dtype), kind="ExternalInput").ap()
            for n, v in arrays.items()}
    out = nc.dram_tensor("out", (N, D), FP32, kind="ExternalOutput").ap()
    graph_layers(nc, **args, out=out)
    r = run_bass_kernel_spmd(nc, [{f"in_{n}": v for n, v in arrays.items()}], core_ids=[0])
    return r.results[0]["out"]
```
